# Optimizing a Trainium2 kernel written in Bass

```python
import numpy as np
import jax
import jax.numpy as jnp

def _softmax(x, axis=-1):
    return jax.nn.softmax(x, axis=axis)

def _gelu(x):
    return jax.nn.gelu(x, approximate=True)

def _silu(x):
    return jax.nn.silu(x)

def _sigmoid(x):
    return jax.nn.sigmoid(x)

def _layernorm(x, axis=-1, eps=1e-05):
    m = jnp.mean(x, axis=axis, keepdims=True)
    v = jnp.var(x, axis=axis, keepdims=True)
    return (x - m) / jnp.sqrt(v + eps)

def _scatter_add(tgt, idx, src, axis=0):
    return tgt.at[idx].add(src)

def _segment_sum(src, seg, n):
    return jax.ops.segment_sum(src, seg, n)
kernel_name = 'mk_gnn_ffn_d1_gnn_r8_f3a2f8'

def setup_inputs(seed: int=0):
    np.random.seed(seed)
    _w = jnp.asarray

    def _rec_inputs():
        import jax
        import jax.numpy as jnp
        _gk = jax.random.key(seed)
        x = -0.0003713 + 1 * jax.random.normal(jax.random.fold_in(_gk, 1), (6250, 256), jnp.float32)
        _s = jax.random.randint(jax.random.fold_in(_gk, 2), (50000,), 0, 6250, jnp.int32)
        _d = jax.random.randint(jax.random.fold_in(_gk, 3), (50000,), 0, 6250, jnp.int32)
        _loop = jnp.arange(6250, dtype=jnp.int32)
        src = jnp.concatenate([_s, _d, _loop])
        dst = jnp.concatenate([_d, _s, _loop])
        _o = jnp.argsort(dst, stable=True)
        src = src[_o]
        dst = dst[_o]
        return (x, src, dst)
    x, src, dst = _rec_inputs()

    def _L0_gnn_setup():
        import jax, jax.numpy as jnp
        import numpy as np
        N = 6250
        E = 100000
        D_IN = 256
        D_H = 512
        D_OUT = 256
        key = jax.random.key(seed)
        ks = jax.random.split(key, 12)
        s = lambda d: 1.0 / np.sqrt(d)
        x = jax.random.normal(ks[0], (N, D_IN), dtype=jnp.float32)
        edge_index = jax.random.randint(ks[1], (2, E), 0, N, dtype=jnp.int64)
        W_rel = jax.random.uniform(ks[2], (D_IN, D_H), jnp.float32, -s(D_IN), s(D_IN))
        b_rel = jax.random.uniform(ks[3], (D_H,), jnp.float32, -s(D_IN), s(D_IN))
        W_root = jax.random.uniform(ks[4], (D_IN, D_H), jnp.float32, -s(D_IN), s(D_IN))
        W_ih = jax.random.uniform(ks[5], (4 * D_H, D_H), jnp.float32, -s(D_H), s(D_H))
        W_hh = jax.random.uniform(ks[6], (4 * D_H, D_H), jnp.float32, -s(D_H), s(D_H))
        b_ih = jax.random.uniform(ks[7], (4 * D_H,), jnp.float32, -s(D_H), s(D_H))
        b_hh = jax.random.uniform(ks[8], (4 * D_H,), jnp.float32, -s(D_H), s(D_H))
        W_fc = jax.random.uniform(ks[9], (D_H, D_OUT), jnp.float32, -s(D_H), s(D_H))
        b_fc = jax.random.uniform(ks[10], (D_OUT,), jnp.float32, -s(D_H), s(D_H))
        return {'x': x, 'edge_index': edge_index, 'W_rel': W_rel, 'b_rel': b_rel, 'W_root': W_root, 'W_ih': W_ih, 'W_hh': W_hh, 'b_ih': b_ih, 'b_hh': b_hh, 'W_fc': W_fc, 'b_fc': b_fc}
    _L0_gnn_all = _L0_gnn_setup()
    _L0_gnn_in = {k: v for k, v in _L0_gnn_all.items() if k in ('W_rel', 'b_rel', 'W_root', 'W_ih', 'W_hh', 'b_ih', 'b_hh', 'W_fc', 'b_fc')}
    del _L0_gnn_all

    def _L0_ffn_setup():
        import jax, jax.numpy as jnp
        import numpy as np
        DIM = 256
        H = 8
        D = 64
        G = 64
        INNER = H * D
        SCALE = D ** (-0.5)
        key = jax.random.key(seed)
        ks = jax.random.split(key, 12)
        B, N = (4, 2048)
        x = jax.random.normal(ks[0], (B, N, DIM), dtype=jnp.float32)
        s = lambda fan_in: 1.0 / np.sqrt(fan_in)
        W_fx = jax.random.normal(ks[1], (DIM, INNER), dtype=jnp.float32) * s(DIM)
        b_fx = jnp.zeros((INNER,), dtype=jnp.float32)
        W_x = jax.random.normal(ks[2], (DIM, INNER), dtype=jnp.float32) * s(DIM)
        b_x = jnp.zeros((INNER,), dtype=jnp.float32)
        A = jax.random.normal(ks[3], (G, D), dtype=jnp.float32)
        Q, _ = jnp.linalg.qr(A.T)
        W_slice = Q[:, :G].astype(jnp.float32)
        b_slice = jnp.zeros((G,), dtype=jnp.float32)
        W_q = jax.random.normal(ks[4], (D, D), dtype=jnp.float32) * s(D)
        W_k = jax.random.normal(ks[5], (D, D), dtype=jnp.float32) * s(D)
        W_v = jax.random.normal(ks[6], (D, D), dtype=jnp.float32) * s(D)
        W_out = jax.random.normal(ks[7], (INNER, DIM), dtype=jnp.float32) * s(INNER)
        b_out = jnp.zeros((DIM,), dtype=jnp.float32)
        temperature = jnp.ones((1, H, 1, 1), dtype=jnp.float32) * 0.5
        return {'x': x, 'W_fx': W_fx, 'b_fx': b_fx, 'W_x': W_x, 'b_x': b_x, 'W_slice': W_slice, 'b_slice': b_slice, 'W_q': W_q, 'W_k': W_k, 'W_v': W_v, 'W_out': W_out, 'b_out': b_out, 'temperature': temperature}
    _L0_ffn_all = _L0_ffn_setup()
    _L0_ffn_in = {k: v for k, v in _L0_ffn_all.items() if k in ('W_fx', 'b_fx', 'W_x', 'b_x', 'W_slice', 'b_slice', 'W_q', 'W_k', 'W_v', 'W_out', 'b_out', 'temperature')}
    del _L0_ffn_all
    return {'x': x, 'src': src, 'dst': dst, 'L0_gnn_W_rel': _L0_gnn_in['W_rel'], 'L0_gnn_b_rel': _L0_gnn_in['b_rel'], 'L0_gnn_W_root': _L0_gnn_in['W_root'], 'L0_gnn_W_ih': _L0_gnn_in['W_ih'], 'L0_gnn_W_hh': _L0_gnn_in['W_hh'], 'L0_gnn_b_ih': _L0_gnn_in['b_ih'], 'L0_gnn_b_hh': _L0_gnn_in['b_hh'], 'L0_gnn_W_fc': _L0_gnn_in['W_fc'], 'L0_gnn_b_fc': _L0_gnn_in['b_fc'], 'L0_ffn_W_fx': _L0_ffn_in['W_fx'], 'L0_ffn_b_fx': _L0_ffn_in['b_fx'], 'L0_ffn_W_x': _L0_ffn_in['W_x'], 'L0_ffn_b_x': _L0_ffn_in['b_x'], 'L0_ffn_W_slice': _L0_ffn_in['W_slice'], 'L0_ffn_b_slice': _L0_ffn_in['b_slice'], 'L0_ffn_W_q': _L0_ffn_in['W_q'], 'L0_ffn_W_k': _L0_ffn_in['W_k'], 'L0_ffn_W_v': _L0_ffn_in['W_v'], 'L0_ffn_W_out': _L0_ffn_in['W_out'], 'L0_ffn_b_out': _L0_ffn_in['b_out'], 'L0_ffn_temperature': _L0_ffn_in['temperature']}

def reference(x, src, dst, L0_gnn_W_rel, L0_gnn_b_rel, L0_gnn_W_root, L0_gnn_W_ih, L0_gnn_W_hh, L0_gnn_b_ih, L0_gnn_b_hh, L0_gnn_W_fc, L0_gnn_b_fc, L0_ffn_W_fx, L0_ffn_b_fx, L0_ffn_W_x, L0_ffn_b_x, L0_ffn_W_slice, L0_ffn_b_slice, L0_ffn_W_q, L0_ffn_W_k, L0_ffn_W_v, L0_ffn_W_out, L0_ffn_b_out, L0_ffn_temperature):
    import jax
    import jax.numpy as jnp

    def _L0_gnn_ref(x, edge_index, W_rel, b_rel, W_root, W_ih, W_hh, b_ih, b_hh, W_fc, b_fc):
        import jax, jax.numpy as jnp
        import numpy as np
        N = 6250
        E = 100000
        D_IN = 256
        D_H = 512
        D_OUT = 256
        src, dst = (edge_index[0], edge_index[1])
        agg = jax.ops.segment_sum(x[src], dst, num_segments=N)
        h = jax.nn.relu(agg @ W_rel + b_rel + x @ W_root)
        gates = h @ W_ih.T + b_ih + b_hh
        i, f, g, o = jnp.split(gates, 4, axis=-1)
        c = jax.nn.sigmoid(i) * jnp.tanh(g)
        h_lstm = jax.nn.sigmoid(o) * jnp.tanh(c)
        return h_lstm @ W_fc + b_fc

    def _L0_ffn_ref(x, W_fx, b_fx, W_x, b_x, W_slice, b_slice, W_q, W_k, W_v, W_out, b_out, temperature):
        import jax, jax.numpy as jnp
        import numpy as np
        DIM = 256
        H = 8
        D = 64
        G = 64
        INNER = H * D
        SCALE = D ** (-0.5)
        B, N, _ = x.shape
        fx_mid = (x @ W_fx + b_fx).reshape(B, N, H, D).transpose(0, 2, 1, 3)
        x_mid = (x @ W_x + b_x).reshape(B, N, H, D).transpose(0, 2, 1, 3)
        temp = jnp.clip(temperature, 0.1, 5.0)
        slice_weights = jax.nn.softmax((x_mid @ W_slice + b_slice) / temp, axis=-1)
        slice_norm = slice_weights.sum(axis=2)
        slice_token = jnp.einsum('bhnc,bhng->bhgc', fx_mid, slice_weights)
        slice_token = slice_token / (slice_norm[..., None] + 1e-05)
        q = slice_token @ W_q
        k = slice_token @ W_k
        v = slice_token @ W_v
        attn = jax.nn.softmax(jnp.einsum('bhgc,bhkc->bhgk', q, k) * SCALE, axis=-1)
        out_slice = jnp.einsum('bhgk,bhkc->bhgc', attn, v)
        out_x = jnp.einsum('bhgc,bhng->bhnc', out_slice, slice_weights)
        out_x = out_x.transpose(0, 2, 1, 3).reshape(B, N, INNER)
        return out_x @ W_out + b_out
    edge_index = jnp.stack([src, dst])
    x = x + _L0_gnn_ref(_layernorm(x, axis=-1), edge_index, L0_gnn_W_rel, L0_gnn_b_rel, L0_gnn_W_root, L0_gnn_W_ih, L0_gnn_W_hh, L0_gnn_b_ih, L0_gnn_b_hh, L0_gnn_W_fc, L0_gnn_b_fc)
    x = x + _L0_ffn_ref(_layernorm(x, axis=-1)[None], L0_ffn_W_fx, L0_ffn_b_fx, L0_ffn_W_x, L0_ffn_b_x, L0_ffn_W_slice, L0_ffn_b_slice, L0_ffn_W_q, L0_ffn_W_k, L0_ffn_W_v, L0_ffn_W_out, L0_ffn_b_out, L0_ffn_temperature)[0]
    return x

_drawn_inputs = setup_inputs


def setup_inputs(seed=0):
    import zlib

    import numpy as np

    out = dict(_drawn_inputs(seed))
    spreads = {'L0_ffn_b_fx': (0.0, 0.1),
     'L0_ffn_b_x': (0.0, 0.8),
     'L0_ffn_b_slice': (0.0, 2.0),
     'L0_ffn_b_out': (0.0, 0.1),
     'L0_ffn_temperature': (0.5, 0.6)}
    factors = {'L0_gnn_b_rel': 8.0,
     'L0_gnn_b_ih': 8.0,
     'L0_gnn_b_hh': 8.0,
     'L0_ffn_W_x': 8.0,
     'L0_ffn_W_slice': 8.0,
     'L0_ffn_W_q': 8.0,
     'L0_ffn_W_k': 8.0}
    for name, (base, spread) in spreads.items():
        noise = np.random.default_rng([zlib.crc32(name.encode()), seed]).standard_normal(out[name].shape)
        drawn = base * np.exp(spread * noise) if base else spread * noise
        out[name] = jnp.asarray(drawn.astype(out[name].dtype))
    for name, factor in factors.items():
        out[name] = (out[name] * factor).astype(out[name].dtype)
    return out
```

```python
from contextlib import ExitStack

import concourse.bass as bass
from concourse import mybir

F32 = mybir.dt.float32
F32R = mybir.dt.float32r
F16 = mybir.dt.float16
I32 = mybir.dt.int32
ALU = mybir.AluOpType
ACT = mybir.ActivationFunctionType
AX = mybir.AxisListType
ds = bass.ds

P = 128
EPS = 1e-5


def build_program(nc, a, out):
    N, C = a["x"].shape
    (E,) = a["src"].shape
    HID = a["W_rel"].shape[1]
    G = a["W_slice"].shape[1]
    D = a["W_slice"].shape[0]
    H = a["temperature"].shape[1]
    HG = H * G
    WN = 125
    NW = N // WN
    NP = NW // 2
    CH = 18
    HALF = CH // 2
    CAP = CH * P
    ROUNDS = -(-E // CAP)
    EP = max(E + CAP, ROUNDS * CAP)
    ER = E // WN
    NOWHERE = 8191
    KT = HID // P
    CT = C // P
    GATES = (0, 2, 3)
    MT = 3 * KT
    SCALE = float(D) ** -0.5
    assert NW * WN == N and 2 * NP == NW and ER * WN == E and N <= NOWHERE

    RP = N // P
    LR = 4
    NCH = RP // LR
    REST = N - RP * P
    assert NCH * LR == RP

    with ExitStack() as ctx:
        def sb(name, shape, dt=F32):
            return ctx.enter_context(nc.sbuf_tensor(name, shape, dt))

        def sem(name):
            return ctx.enter_context(nc.semaphore(name))

        def dram(name, shape, dt):
            return nc.dram_tensor(name, shape, dt).ap()

        table = dram("table", [N, 2 * C], F16)
        srcp = dram("srcp", [EP], I32)
        dstp = dram("dstp", [EP], I32)
        sums = dram("sums", [N, C], F32)
        res = dram("res", [N, C], F32)
        swt_d = dram("swt_d", [NP, P, 2 * KT * WN], F32)

        wih_h = sb("wih_h", [P, KT, MT, P], F32R)
        wih_l = sb("wih_l", [P, KT, MT, P], F32R)
        w1_h = sb("w1_h", [P, 2 * CT, HID], F32R)
        w1_l = sb("w1_l", [P, 2 * CT, HID], F32R)
        wfc_h = sb("wfc_h", [P, KT, C], F32R)
        wfc_l = sb("wfc_l", [P, KT, C], F32R)
        wxs_h = sb("wxs_h", [P, CT, HG], F32R)
        wxs_l = sb("wxs_l", [P, CT, HG], F32R)
        ring = sb("ring", [P, 2, CH, 2 * C], F16)
        oneh = sb("oneh", [P, 2, CH, P], F16)
        hf = sb("hf", [P, KT, 2 * P])
        h_h = sb("h_h", [P, KT, 2 * P], F32R)
        h_l = sb("h_l", [P, KT, 2 * P], F32R)
        hl_h = sb("hl_h", [P, KT, 2 * P], F32R)
        hl_l = sb("hl_l", [P, KT, 2 * P], F32R)
        at_h = sb("at_h", [P, CT, 2 * P], F32R)
        at_l = sb("at_l", [P, CT, 2 * P], F32R)
        xt_h = sb("xt_h", [P, CT, 2 * P], F32R)
        xt_l = sb("xt_l", [P, CT, 2 * P], F32R)
        agg = sb("agg", [P, 2, C])
        xn16 = sb("xn16", [P, 2, 2 * C], F16)
        xin = sb("xin", [P, 2, C])
        x2 = sb("x2", [P, 2, C])
        x2_h = sb("x2_h", [P, 2, C], F32R)
        x2_l = sb("x2_l", [P, 2, C], F32R)
        x2t_h = sb("x2t_h", [P, CT, 2 * P], F32R)
        x2t_l = sb("x2t_l", [P, CT, 2 * P], F32R)
        gate = sb("gate", [P, 3, KT, 2 * P])
        sw = sb("sw", [P, 2, HG])
        sw_h = sb("sw_h", [P, 2, HG], F32R)
        sw_l = sb("sw_l", [P, 2, HG], F32R)
        norm = sb("norm", [P, HG])
        swt = sb("swt", [P, 2, KT, WN])
        biasx = sb("biasx", [P, HG])
        ident = sb("ident", [P, P])
        ident16 = sb("ident16", [P, P], F16)
        iota = sb("iota", [P, P], F16)
        wbase = sb("wbase", [P, NW + 2])
        rel = sb("rel", [P, 2, CH])
        sidx = sb("sidx", [P, 2, CH], I32)
        didx = sb("didx", [P, 2, CH], I32)
        ones = sb("ones", [P, 1])
        bfc = sb("bfc", [P, C])
        bout = sb("bout", [P, C])
        brel = sb("brel", [P, KT])
        bgate = sb("bgate", [P, KT, 3])
        braw = sb("braw", [P, 2, 3, KT])
        temp8 = sb("temp8", [P, H])
        rtemp = sb("rtemp", [P, H])
        extra = sb("extra", [P, 2, C])
        stats = sb("stats", [P, 2, LR, 6])
        mv = sb("mv", [P, 2, LR, 2])
        sd = sb("sd", [P, 2, LR])
        rstd = sb("rstd", [P, 2, LR])
        nmr = sb("nmr", [P, 2, LR])
        eps = sb("eps", [P, 1])
        mx8 = sb("mx8", [P, 2 * H])
        sm8 = sb("sm8", [P, 2 * H])
        rs8 = sb("rs8", [P, 2 * H])
        base_i = sb("base_i", [1, NW + 2], I32)
        flag_i = sb("flag_i", [1, 1], I32)
        col = sb("col", [P, 8])
        coli = sb("coli", [P, 1], I32)

        scratch = ring[:, :, :, :].rearrange("p a b c -> p (a b c)").bitcast(F32)
        words = LR * C
        lx = [scratch[:, k * words:(k + 1) * words].rearrange("p (r c) -> p r c", c=C) for k in range(3)]
        ln = [scratch[:, (3 + k) * words:(4 + k) * words].rearrange("p (r c) -> p r c", c=C) for k in range(2)]
        lt = [scratch[:, (5 + k) * words:(6 + k) * words].bitcast(F16).rearrange("p (r c) -> p r c", c=2 * C)
              for k in range(2)]
        edge_i = scratch[:, 7 * words:7 * words + ER + 1].bitcast(I32)
        row = scratch[0:1, 8100:8100 + 5 * (NW + 2)].rearrange("p (k n) -> p k n", k=5)
        pick = scratch[:, 8400:8400 + NW + 2]
        hot_words = oneh[:, :, :, :].rearrange("p a b c -> p (a b c)").bitcast(F32)
        edge_f = hot_words[:, 0:ER + 1]
        edge_le = hot_words[:, 1000:1000 + ER]
        raw = gate[:, :, :, :].rearrange("p a b c -> p (a b c)")
        wx_raw = sw[:, :, :]
        wxt = hf[:, :, :]
        wsl = swt[:, :, :, :].rearrange("p a b c -> p (a b c)")[:, 0:G]
        bsl = swt[:, :, :, :].rearrange("p a b c -> p (a b c)")[:, 64:64 + G]
        bxc = swt[:, :, :, :].rearrange("p a b c -> p (a b c)")[:, 128:128 + KT]
        bxb = swt[:, :, :, :].rearrange("p a b c -> p (a b c)")[:, 256:256 + KT * P].rearrange(
            "p (k n) -> p k n", n=P)

        at = 0

        def carve(parts, n):
            nonlocal at
            at += n
            assert at <= 9216
            return scratch[0:parts, at - n:at]

        wfx = carve(P, CT * HG).rearrange("p (k n) -> p k n", k=CT)
        tks = carve(P, CT * HG).rearrange("p (k n) -> p k n", k=CT)
        wout = carve(D, H * C).rearrange("p (h n) -> p h n", h=H)
        wqkv = carve(D, 3 * D).rearrange("p (k n) -> p k n", k=3)
        bfx, tokens, tokt, qt, kt, vv, att, attt, tmp = (carve(G, HG) for _ in range(9))
        ost = tokens
        fsw = [raw[:, k * 1024:k * 1024 + 2 * KT * WN] for k in range(2)]
        fres = hf[:, :, :].rearrange("p a b -> p (a b)").rearrange("p (k e c) -> p k e c", k=2, e=2)
        fo = sw[:, :, :]
        wih_hf, wih_lf = (w[:, :, :, :].rearrange("p a b c -> p (a b c)") for w in (wih_h, wih_l))
        fsw_h, fsw_l = ([w[:, k * 1024:k * 1024 + 2 * KT * WN] for k in range(2)] for w in (wih_hf, wih_lf))
        v_h, v_l = (w[:, 2048:3072].rearrange("p (j c) -> p j c", c=C) for w in (wih_hf, wih_lf))

        ps = ctx.enter_context(nc.psum_tensor("ps", [P, 8, 512], F32))
        SUM_A, SUM_B, XA, XX, HA, HB, TOK = 0, 1, 2, 3, 4, 5, 6
        xx16 = ps[:, XX, :].bitcast(F16).rearrange("p (h q n) -> p h q n", h=2, q=2)

        ld_edges, ld_pads, ld_tab = sem("ld_edges"), sem("ld_pads"), sem("ld_tab")
        ld_small, ld_w1, ld_wih, ld_wx, ld_wfc = (sem(n) for n in ("ld_small", "ld_w1", "ld_wih", "ld_wx", "ld_wfc"))
        ld_rows = sem("ld_rows")
        ln_in = [sem(f"ln_in{k}") for k in range(3)]
        ln_out = [sem(f"ln_out{k}") for k in range(2)]
        consts, dve_step, act_step, pe_step, pool_step = (
            sem(n) for n in ("consts", "dve_step", "act_step", "pe_step", "pool_step"))
        pads_set, plan_m, plan_pw, plan_row, plan_cnt, plan_t, plan_done = (
            sem(n) for n in ("pads_set", "plan_m", "plan_pw", "plan_row", "plan_cnt", "plan_t", "plan_done"))
        ln_var, ln_sd, ln_rstd, ln_x, ln_hi, ln_lo = (
            sem(n) for n in ("ln_var", "ln_sd", "ln_rstd", "ln_x", "ln_hi", "ln_lo"))
        w1_free, wprep_t, wprep_h, wprep_l, wxt_t, wxt_c, wxs_m, wxs_c, bx_set, bx_m, w_ready = (
            sem(n) for n in ("w1_free", "wprep_t", "wprep_h", "wprep_l", "wxt_t", "wxt_c", "wxs_m", "wxs_c",
                             "bx_set", "bx_m", "w_ready"))
        tok_zero = sem("tok_zero")
        gather_go = sem("gather_go")
        gen_idx, gen_rel, gen_hot, gen_rows, gen_mm, gen_zero, gen_sum, gen_st = (
            sem(n) for n in ("gen_idx", "gen_rel", "gen_hot", "gen_rows", "gen_mm", "gen_zero", "gen_sum", "gen_st"))
        idx_in = [sem(f"idx_in{e}") for e in range(2)]
        rel_done = [sem(f"rel_done{e}") for e in range(2)]
        hot_done = [sem(f"hot_done{e}") for e in range(2)]
        rows_in = [[sem(f"rows_in{e}{k}") for k in range(2)] for e in range(2)]
        half_used = [sem(f"half_used{e}") for e in range(2)]
        sum_done = [sem(f"sum_done{e}") for e in range(2)]
        agg_done = [sem(f"agg_done{e}") for e in range(2)]
        gen_in = sem("gen_in")
        xn_in, x_in = sem("xn_in"), sem("x_in")
        xt_done, xsplit_a, xsplit_v = sem("xt_done"), sem("xsplit_a"), sem("xsplit_v")
        h_mm, h_act, h_hi, h_lo = sem("h_mm"), sem("h_act"), sem("h_hi"), sem("h_lo")
        gate_mm, gate_act, cell_v, cell_t, cell_out, hl_hi, hl_lo = (
            sem(n) for n in ("gate_mm", "gate_act", "cell_v", "cell_t", "cell_out", "hl_hi", "hl_lo"))
        y_mm, x2_step, var_done, sd_done, rstd_done, res_done, res_st = (
            sem(n) for n in ("y_mm", "x2_step", "var_done", "sd_done", "rstd_done", "res_done", "res_st"))
        x2_norm, x2_hi, x2_lo, x2t_mm, x2t_hi, x2t_lo = (
            sem(n) for n in ("x2_norm", "x2_hi", "x2_lo", "x2t_mm", "x2t_hi", "x2t_lo"))
        lg_mm, lg_sub, lg_exp, sm_step, sw_done, norm_add, sw_hi, sw_lo = (
            sem(n) for n in ("lg_mm", "lg_sub", "lg_exp", "sm_step", "sw_done", "norm_add", "sw_hi", "sw_lo"))
        swt_mm, swt_done, swt_st, tok_mm = sem("swt_mm"), sem("swt_done"), sem("swt_st"), sem("tok_mm")
        ld_att, att_pe, att_v, att_a = sem("ld_att"), sem("att_pe"), sem("att_v"), sem("att_a")
        f_in = [sem(f"f_in{k}") for k in range(2)]
        f_res = [sem(f"f_res{k}") for k in range(2)]
        f_st = [sem(f"f_st{k}") for k in range(2)]
        f_hi = [sem(f"f_hi{k}") for k in range(2)]
        f_lo = [sem(f"f_lo{k}") for k in range(2)]
        f_mm = [sem(f"f_mm{k}") for k in range(2)]
        f_out = [sem(f"f_out{k}") for k in range(2)]

        gen_rel2, gen_add = sem("gen_rel2"), sem("gen_add")
        low_out = [sem(f"low_out{e}") for e in range(2)]
        V_TKS, V_TOKENS, V_TOKT, V_QKV, ATT_SUB, V_ATT, V_ATTT, V_OST, V_VLO = 1, 7, 8, 11, 13, 16, 17, 18, 20
        PE_V = 8

        block = ctx.enter_context(nc.Block())

        def pair_rows(t, p, width):
            return t[ds(p * (2 * WN), 2 * WN), :].rearrange("(e n) c -> n e c", n=WN)

        PARTS = ((0, 112), (112, WN))

        def turns(turn):
            turn(0, True, False, False, True)
            turn(1, True, True, False, True)
            return (2, NP - 1)

        def last_turns(turn):
            turn(NP - 1, True, True, True, False)
            turn(NP, False, True, True, False)
            turn(NP + 1, False, False, True, False)

        def three(eng, dst, wh, wl, xh, xl, first, last):
            eng.matmul(dst, wh, xh, start=first, stop=False)
            eng.matmul(dst, wh, xl, start=False, stop=False)
            return eng.matmul(dst, wl, xh, start=False, stop=last)


        @block.sync
        def _(sp):
            sp.dma_start(srcp[0:E].rearrange("(a b) -> a b", b=ER), a["src"].rearrange("(a b) -> a b", b=ER)).then_inc(ld_edges, 16)
            sp.dma_start(dstp[0:E].rearrange("(a b) -> a b", b=ER), a["dst"].rearrange("(a b) -> a b", b=ER)).then_inc(ld_edges, 16)

            def load_chunk(k):
                if k >= 3:
                    sp.wait_ge(ln_x, LR * (k - 2))
                if k < NCH:
                    src = a["x"][0:RP * P, :].rearrange("(p r) c -> p r c", p=P)[:, k * LR:(k + 1) * LR, :]
                    sp.dma_start(lx[k % 3], src).then_inc(ln_in[k % 3], 16)
                else:
                    sp.dma_start(lx[k % 3][0:REST, 0, :], a["x"][RP * P:N, :]).then_inc(ln_in[k % 3], 16)

            def store_chunk(k):
                sp.wait_ge(ln_hi, k + 1)
                sp.wait_ge(ln_lo, k + 1)
                if k < NCH:
                    dst = table[0:RP * P, :].rearrange("(p r) c -> p r c", p=P)[:, k * LR:(k + 1) * LR, :]
                    sp.dma_start(dst, lt[k % 2]).then_inc(ln_out[k % 2], 16)
                else:
                    sp.dma_start(table[RP * P:N, :], lt[k % 2][0:REST, 0, :]).then_inc(ln_out[k % 2], 16)

            load_chunk(0)
            load_chunk(1)
            load_chunk(2)
            with nc.allow_non_contiguous_dma(reason="bias vectors go down the partitions once"):
                sp.dma_start(brel[:, :], a["b_rel"].rearrange("(k p) -> p k", p=P)).then_inc(ld_small, 16)
                for j, g in enumerate(GATES):
                    for q, b in enumerate(("b_ih", "b_hh")):
                        v = a[b][g * HID:(g + 1) * HID].rearrange("(k p) -> p k", p=P)
                        sp.dma_start(braw[:, q, j, :], v).then_inc(ld_small, 16)
                sp.dma_start(bxc, a["b_x"].rearrange("(k p) -> p k", p=P)).then_inc(ld_small, 16)
            sp.dma_start(bfc[:, :], a["b_fc"].partition_broadcast(P)).then_inc(ld_small, 16)
            sp.dma_start(bout[:, :], a["b_out"].partition_broadcast(P)).then_inc(ld_small, 16)
            sp.dma_start(bsl, a["b_slice"].partition_broadcast(P)).then_inc(ld_small, 16)
            sp.dma_start(temp8[:, :], a["temperature"].rearrange("a h b c -> (a h b c)").partition_broadcast(P)).then_inc(ld_small, 16)
            for k in range(2):
                sp.dma_start(wsl[k * D:(k + 1) * D, :], a["W_slice"]).then_inc(ld_small, 16)
            sp.dma_start(wx_raw, a["W_x"].rearrange("(k p) n -> p k n", p=P)).then_inc(ld_wx, 16)
            sp.wait_ge(pads_set, 2)
            for idx, t in ((sidx, srcp), (didx, dstp)):
                sp.dma_start(t[E:EP].rearrange("(p b) -> p b", p=P), idx[:, 0, :]).then_inc(ld_pads, 16)
            sp.wait_ge(ld_edges, 32)
            sp.wait_ge(ld_pads, 32)
            rows = dstp[0:E].rearrange("(p b) -> p b", b=ER)
            nxt = dstp[ER:E + ER].rearrange("(p b) -> p b", b=ER)
            sp.dma_start(edge_i[0:WN, 0:ER], rows).then_inc(ld_tab, 16)
            with nc.allow_non_contiguous_dma(reason="one element a row"):
                sp.dma_start(edge_i[0:WN, ER:ER + 1], nxt[:, 0:1]).then_inc(ld_tab, 16)
            r4 = raw[:, 0:4 * HID].rearrange("p (k n) -> p k n", n=HID)
            for k in range(NCH + 1):
                if k + 3 <= NCH:
                    load_chunk(k + 3)
                if k >= 1:
                    store_chunk(k - 1)
                if k == NCH - 2:
                    sp.dma_start(r4[:, 0:CT, :], a["W_rel"].rearrange("(k p) n -> p k n", p=P)).then_inc(ld_w1, 16)
                    sp.dma_start(r4[:, CT:2 * CT, :], a["W_root"].rearrange("(k p) n -> p k n", p=P)).then_inc(ld_w1, 16)
            store_chunk(NCH)

            sp.wait_ge(plan_done, 2)
            general = sp.value_load(flag_i[0:1, 0:1], min_val=0, max_val=1)

            def load_edges(base, e, done):
                for idx, t in ((sidx, srcp), (didx, dstp)):
                    sp.dma_start(idx[:, e, :], t[ds(base, CAP)].rearrange("(p j) -> p j", p=P)).then_inc(done, 16)

            with sp.If(general):
                sp.sem_inc(gen_st, 16)
                with sp.Fori(0, NW) as w:
                    with sp.Fori(0, ROUNDS) as r:
                        sp.wait_ge(gen_mm, w * ROUNDS + r + 1)
                        load_edges(r * CAP, 0, gen_idx)
                    sp.wait_ge(gen_sum, w + 2)
                    sp.dma_start(sums[ds(w * WN, WN), :], agg[0:WN, 0, :]).then_inc(gen_st, 16)
                sp.wait_ge(gen_st, 16 * NW + 16)

            def edges(p, e):
                w = 2 * p + e
                if not (isinstance(p, int) and p == 0):
                    sp.wait_ge(rows_in[e][0], 16 * HALF * p)
                    sp.wait_ge(rows_in[e][1], 16 * HALF * p)
                    sp.wait_ge(rel_done[e], p)
                base = sp.value_load(base_i[0:1, ds(w, 1)], min_val=0, max_val=E)
                load_edges(base, e, idx_in[e])

            def turn(t, gather, gnn, ffn, ahead):
                if gather:
                    if not (isinstance(t, int) and t == 0):
                        sp.wait_ge(xt_done, t)
                    for u, v in PARTS:
                        sp.dma_start(xn16[u:v, :, :], pair_rows(table, t, 2 * C)[u:v]).then_inc(xn_in, 16)
                    with sp.If(general):
                        sp.wait_ge(gen_add, 2 * t)
                        for u, v in PARTS:
                            sp.dma_start(extra[u:v], pair_rows(sums, t, C)[u:v]).then_inc(gen_in, 16)
                if ahead:
                    edges(t + 1, 0)
                if ffn:
                    p = t - 2
                    sp.wait_ge(res_done, p + 1)
                    for u, v in PARTS:
                        sp.dma_start(pair_rows(res, p, C)[u:v], xin[u:v, :, :]).then_inc(res_st, 16)
                if gnn:
                    p = t - 1
                    if not (isinstance(p, int) and p == 0):
                        sp.wait_ge(res_st, 32 * p)
                    for u, v in PARTS:
                        sp.dma_start(xin[u:v, :, :], pair_rows(a["x"], p, C)[u:v]).then_inc(x_in, 16)
                if ahead:
                    edges(t + 1, 1)

            edges(0, 0)
            edges(0, 1)
            sp.wait_ge(w1_free, 2)
            for q in range(2):
                if q:
                    sp.wait_ge(wprep_t, MT // 2)
                for n in range(q * MT // 2, (q + 1) * MT // 2):
                    f, g = n // 3, GATES[n % 3]
                    r = g * HID + f * P
                    s = n % (MT // 2)
                    sp.dma_start(raw[:, s * HID:(s + 1) * HID], a["W_ih"][r:r + P, :]).then_inc(ld_wih, 16)
            sp.wait_ge(wprep_t, MT)
            sp.dma_start(raw[:, 0:KT * C].rearrange("p (k n) -> p k n", n=C),
                         a["W_fc"].rearrange("(k p) n -> p k n", p=P)).then_inc(ld_wfc, 16)
            lo, hi = turns(turn)
            with sp.Fori(lo, hi) as t:
                turn(t, True, True, True, True)
            last_turns(turn)
            sp.wait_ge(res_st, 32 * NP)
            sp.wait_ge(swt_st, 16 * NP)

            sp.wait_ge(sum_done[1], NP)
            sp.dma_start(wfx, a["W_fx"].rearrange("(k p) n -> p k n", p=P)).then_inc(ld_att, 16)
            sp.dma_start(wout, a["W_out"].rearrange("(h p) n -> p h n", p=D)).then_inc(ld_att, 16)
            for k, n in enumerate(("W_q", "W_k", "W_v")):
                sp.dma_start(wqkv[:, k, :], a[n]).then_inc(ld_att, 16)
            sp.dma_start(bfx, a["b_fx"].partition_broadcast(G)).then_inc(ld_att, 16)

            def f_load_weights(n, k):
                p = 2 * n + k
                if not (isinstance(n, int) and n == 0):
                    sp.wait_ge(f_hi[k], n)
                    sp.wait_ge(f_lo[k], n)
                sp.dma_start(fsw[k], swt_d[ds(p, 1)].rearrange("a p n -> p (a n)")).then_inc(f_in[k], 16)

            def f_load_rows(n, k):
                p = 2 * n + k
                if not (isinstance(n, int) and n == 0):
                    sp.wait_ge(f_out[k], n + 1)
                for u, v in PARTS:
                    sp.dma_start(fres[u:v, k, :, :], pair_rows(res, p, C)[u:v]).then_inc(f_res[k], 16)

            sp.wait_ge(cell_out, KT * NP)
            sp.wait_ge(hl_lo, 2 * NP)
            for load in (f_load_weights, f_load_rows):
                for k in range(2):
                    load(0, k)
            with sp.Fori(1, NP // 2) as n:
                for load in (f_load_weights, f_load_rows):
                    for k in range(2):
                        load(n, k)
            f_load_weights(NP // 2, 0)
            f_load_rows(NP // 2, 0)
            for k, cnt in ((0, NP - NP // 2), (1, NP // 2)):
                sp.wait_ge(f_st[k], 32 * cnt)

        def after(eng, s, n):
            if not (isinstance(n, int) and n <= 0):
                eng.wait_ge(s, n)

        def valid(x):
            return x.rearrange("p k (e n) -> p (k e) n", n=P)[:, :, 0:WN]

        def bank_valid(b):
            return ps[:, b, :].rearrange("p (q n) -> p q n", n=P)[:, :, 0:WN]

        NCONST = 8

        @block.gpsimd
        def _(pool):
            pool.memset(ident[:, :], 0.0).then_inc(pool_step, 1)
            pool.iota(iota[:, :], [[1, P]], base=0, channel_multiplier=0,
                      allow_small_or_imprecise_dtypes=True).then_inc(consts, 1)
            pool.iota(wbase[:, :], [[WN, NW + 2]], base=0, channel_multiplier=0,
                      allow_small_or_imprecise_dtypes=True).then_inc(consts, 1)
            pool.iota(col[:, 7:8], [[0, 1]], base=0, channel_multiplier=WN,
                      allow_small_or_imprecise_dtypes=True).then_inc(consts, 1)
            pool.memset(ones[:, :], 1.0).then_inc(consts, 1)
            pool.memset(eps[:, :], EPS).then_inc(consts, 1)
            pool.iota(sidx[:, 0, :], [[0, CH]], base=0, channel_multiplier=0).then_inc(pads_set, 1)
            pool.iota(didx[:, 0, :], [[0, CH]], base=NOWHERE, channel_multiplier=0).then_inc(pads_set, 1)
            pool.wait_ge(pool_step, 1)
            pool.affine_select(out=ident[:, :], in_=ident[:, :], compare_op=ALU.not_equal, fill=1.0,
                               base=0, pattern=[[-1, P]], channel_multiplier=1).then_inc(consts, 1)
            for x in (at_h, at_l, xt_h, xt_l):
                pool.memset(x[:, :, :].bitcast(F32), 0.0).then_inc(w_ready, 1)
            pool.memset(norm[:, :], 0.0).then_inc(consts, 1)
            pool.memset(pick[:, :], 0.0).then_inc(consts, 1)

            pool.wait_ge(plan_row, 1)
            pool.indirect_dma_start(edge_i[0:NW + 1, 0:ER], None, dstp[0:E].rearrange("(p b) -> p b", b=ER),
                                    bass.IndirectOffsetOnAxis(ap=coli[0:NW + 1, 0:1], axis=0)).then_inc(ld_rows, 16)
            pool.wait_ge(ln_out[0], 16 * ((NCH + 2) // 2))
            pool.wait_ge(ln_out[1], 16 * ((NCH + 1) // 2))
            pool.wait_ge(plan_done, 2)
            general = pool.value_load(flag_i[0:1, 0:1], min_val=0, max_val=1)

            def gather(e, j, done):
                pool.indirect_dma_start(ring[:, e, j, :], None, table,
                                        bass.IndirectOffsetOnAxis(ap=sidx[:, e, j:j + 1], axis=0)).then_inc(done, 16)

            with pool.If(general):
                with pool.Fori(0, NW) as w:
                    with pool.Fori(0, ROUNDS) as r:
                        n = w * ROUNDS + r
                        pool.wait_ge(gen_idx, n * 32 + 32)
                        pool.wait_ge(gen_mm, n + 1)
                        pool.sem_inc(gather_go, 1)
                        for j in range(CH):
                            gather(0, j, gen_rows)
                pool.wait_ge(gen_mm, NW * ROUNDS + 1)

            def gathers(p):
                for e in range(2):
                    for k, used in enumerate((half_used[e], sum_done[e])):
                        if k == 0:
                            pool.wait_ge(idx_in[e], 32 * p + 32)
                        after(pool, used, p)
                        pool.sem_inc(gather_go, 1)
                        for j in range(k * HALF, (k + 1) * HALF):
                            gather(e, j, rows_in[e][k])

            gathers(0)
            with pool.Fori(1, NP) as p:
                gathers(p)

            def f_store(n, k):
                p = 2 * n + k
                pool.wait_ge(f_out[k], n + 2)
                for u, v in PARTS:
                    pool.dma_start(pair_rows(out, p, C)[u:v],
                                   fo[u:v, k, :].rearrange("p (e c) -> p e c", e=2)).then_inc(f_st[k], 16)

            with pool.Fori(0, NP // 2) as n:
                f_store(n, 0)
                f_store(n, 1)
            f_store(NP // 2, 0)
            for k, cnt in ((0, NP - NP // 2), (1, NP // 2)):
                pool.wait_ge(f_st[k], 32 * cnt)

        @block.scalar
        def _(act):
            act.wait_ge(consts, NCONST)
            def ln_dev(k):
                n, rows = (P, LR) if k < NCH else (REST, 1)
                act.wait_ge(ln_var, k + 1)
                act.activation(sd[0:n, k % 2, 0:rows], mv[0:n, k % 2, 0:rows, 1], ACT.Sqrt,
                               bias=eps[0:n, :]).then_inc(ln_sd, 1)

            ln_dev(0)
            for k in range(NCH + 1):
                n, rows = (P, LR) if k < NCH else (REST, 1)
                q = k % 2
                act.wait_ge(ln_rstd, k + 1)
                if k >= 2:
                    act.wait_ge(ln_hi, k - 1)
                    act.wait_ge(ln_lo, k - 1)
                for r in range(rows):
                    act.activation(ln[q][0:n, r, :], lx[k % 3][0:n, r, :], ACT.Identity,
                                   bias=nmr[0:n, q, r:r + 1], scale=rstd[0:n, q, r:r + 1]).then_inc(ln_x, 1)
                if k < NCH:
                    ln_dev(k + 1)
                act.wait_ge(ln_x, min(LR * (k + 1), LR * NCH + 1))
                if k >= 2:
                    act.wait_ge(ln_out[q], 16 * (k // 2))
                act.activation(lt[q][0:n, 0:rows, 0:C], ln[q][0:n, 0:rows, :], ACT.Copy).then_inc(ln_hi, 1)
            act.wait_ge(ld_w1, 32)
            act.activation(w1_h[:, :, :], raw[:, 0:4 * HID].rearrange("p (k n) -> p k n", n=HID), ACT.Copy).then_inc(w1_free, 1)
            act.wait_ge(wxs_c, 2)
            act.activation(wxs_h[:, :, :], sw[:, :, :], ACT.Copy).then_inc(wprep_h, 1)
            for n in range(MT):
                act.wait_ge(wprep_t, n + 1)
                act.activation(wih_h[:, :, n, :], ps[:, XA + n % 2, :].rearrange("p (k m) -> p k m", m=P),
                               ACT.Copy).then_inc(wprep_h, 1)
            act.wait_ge(ld_wfc, 16)
            act.activation(wfc_h[:, :, :], raw[:, 0:KT * C].rearrange("p (k n) -> p k n", n=C), ACT.Copy,
                           scale=0.5).then_inc(wprep_h, 1)

            def split_x(p):
                act.wait_ge(xt_done, p + 1)
                act.activation(valid(at_h[:, :, :]), bank_valid(XA), ACT.Copy).then_inc(xsplit_a, 1)
                for q, x in enumerate((xt_h, xt_l)):
                    for hh in range(CT):
                        act.activation(x[:, hh, :].rearrange("p (e n) -> p e n", n=P)[:, :, 0:WN],
                                       xx16[:, hh, q, :].rearrange("p (e n) -> p e n", n=P)[:, :, 0:WN],
                                       ACT.Copy).then_inc(xsplit_a, 1)

            def dev_x2(p):
                act.wait_ge(var_done, 2 * p + 2)
                act.activation(sd[0:WN, 0, 0:2], mv[0:WN, 0, 0:2, 1], ACT.Sqrt, bias=eps[0:WN, :]).then_inc(sd_done, 1)

            def norm_x2(p):
                act.wait_ge(rstd_done, 2 * p + 2)
                act.wait_ge(res_done, p + 1)
                for e in range(2):
                    act.activation(x2[0:WN, e, :], x2[0:WN, e, :], ACT.Identity,
                                   bias=nmr[0:WN, 0, e:e + 1], scale=rstd[0:WN, 0, e:e + 1]).then_inc(x2_norm, 1)
                act.wait_ge(x2_norm, 2 * p + 2)
                after(act, tok_mm, p)
                act.activation(x2_h[0:WN, :, :], x2[0:WN, :, :], ACT.Copy).then_inc(x2_hi, 1)

            def relu_h(p, q):
                if q == 0:
                    after(act, hl_lo, 2 * p)
                act.wait_ge(h_mm, 2 * p + q + 1)
                for m in (2 * q, 2 * q + 1):
                    act.activation(hf[:, m, :], ps[:, HA + q, (m % 2) * 256:(m % 2) * 256 + 256], ACT.Relu,
                                   bias=brel[:, m:m + 1]).then_inc(h_act, 1)
                act.wait_ge(h_act, KT * p + 2 * q + 2)
                act.activation(h_h[:, 2 * q:2 * q + 2, :], hf[:, 2 * q:2 * q + 2, :], ACT.Copy).then_inc(h_hi, 1)

            def split_x2t(p):
                act.wait_ge(x2t_mm, p + 1)
                act.activation(valid(x2t_h[:, :, :]), bank_valid(XX), ACT.Copy).then_inc(x2t_hi, 1)

            def gates(p, first, end):
                for n in range(first, end):
                    f, g = n // 3, n % 3
                    act.wait_ge(gate_mm, MT // 2 * p + n // 2 + 1)
                    if n == 0:
                        after(act, cell_out, KT * p)
                    s = n % 4
                    act.activation(gate[:, g, f, :], ps[:, HA + s // 2, (s % 2) * 256:(s % 2) * 256 + 256], ACT.Tanh,
                                   bias=bgate[:, f, g:g + 1], scale=1.0 if g == 1 else 0.5).then_inc(gate_act, 1)

            def tanh_c(p, f):
                act.wait_ge(cell_v, KT * p + f + 1)
                act.activation(gate[:, 1, f, :], gate[:, 0, f, :], ACT.Tanh, scale=0.5).then_inc(cell_t, 1)

            def high_hl(p, q):
                if q == 0:
                    after(act, y_mm, p)
                act.wait_ge(cell_out, KT * p + 2 * q + 2)
                act.activation(hl_h[:, 2 * q:2 * q + 2, :], hf[:, 2 * q:2 * q + 2, :], ACT.Copy).then_inc(hl_hi, 1)

            def turn(t, gather, gnn, ffn, ahead):
                if gnn:
                    split_x(t - 1)
                    relu_h(t - 1, 0)
                if ffn:
                    dev_x2(t - 2)
                if gnn:
                    relu_h(t - 1, 1)
                if ffn:
                    norm_x2(t - 2)
                    split_x2t(t - 2)
                if gnn:
                    gates(t - 1, 0, 4)
                    tanh_c(t - 1, 0)
                    gates(t - 1, 4, 6)
                    tanh_c(t - 1, 1)
                if ffn:
                    act.wait_ge(lg_sub, t - 1)
                    act.activation(sw[0:WN, :, :], sw[0:WN, :, :], ACT.Exp).then_inc(lg_exp, 1)
                if gnn:
                    gates(t - 1, 6, 10)
                if ffn:
                    p = t - 2
                    act.wait_ge(sw_done, p + 1)
                    after(act, tok_mm, p)
                    act.activation(sw_h[0:WN, :, :], sw[0:WN, :, :], ACT.Copy).then_inc(sw_hi, 1)
                if gnn:
                    tanh_c(t - 1, 2)
                    gates(t - 1, 10, 12)
                if ffn:
                    p = t - 2
                    after(act, swt_st, 16 * p)
                    for e in range(2):
                        act.wait_ge(swt_mm, 2 * p + e + 1)
                        act.activation(swt[:, e, :, :], bank_valid(XA + e), ACT.Copy).then_inc(swt_done, 1)
                if gnn:
                    tanh_c(t - 1, 3)
                    high_hl(t - 1, 0)
                    high_hl(t - 1, 1)
                if ffn:
                    act.wait_ge(swt_done, 2 * p + 2)
                    act.dma_start(swt_d[ds(p, 1)].rearrange("a p n -> p (a n)"),
                                  swt[:, :, :, :].rearrange("p e j n -> p (e j n)")).then_inc(swt_st, 16)

            lo, hi = turns(turn)
            with act.Fori(lo, hi) as t:
                turn(t, True, True, True, True)
            last_turns(turn)

            act.wait_ge(att_v, ATT_SUB)
            act.activation(att[:, :], att[:, :], ACT.Exp, scale=SCALE).then_inc(att_a, 1)
            act.wait_ge(att_pe, PE_V)
            for b in range(2):
                act.activation(v_h[:, 2 * b:2 * b + 2, :], ps[:, 3 + b, :].rearrange("p (j c) -> p j c", c=C),
                               ACT.Copy).then_inc(att_a, 1)

            def f_high(n, k):
                act.wait_ge(f_in[k], 16 * n + 16)
                act.wait_ge(f_mm[k], n + 1)
                act.activation(fsw_h[k], fsw[k], ACT.Copy).then_inc(f_hi[k], 1)

            with act.Fori(0, NP // 2) as n:
                f_high(n, 0)
                f_high(n, 1)
            f_high(NP // 2, 0)

        @block.tensor
        def _(pe):
            pe.wait_ge(consts, NCONST)
            pe.wait_ge(w_ready, 4)
            zeros = at_h[:, :, :].rearrange("p k n -> p (k n)")
            for b in (TOK, TOK + 1):
                pe.matmul(ps[:, b, :], zeros[:, 0:P], zeros, start=True, stop=False).then_inc(tok_zero, 1)
            pe.wait_ge(plan_m, 2)
            pe.matmul(ps[0:NW + 1, 0, 0:1], pick[0:WN, 0:NW + 1], ones[0:WN, 0:1], start=True, stop=True)
            pe.matmul(ps[0:1, 1, 0:1], col[0:WN, 0:1], ones[0:WN, 0:1], start=True, stop=True).then_inc(plan_pw, 1)
            pe.wait_ge(ld_wx, 16)
            for ct in range(CT):
                for j in range(KT):
                    last = pe.transpose(ps[:, XA + ct, j * P:(j + 1) * P], wx_raw[:, ct, j * P:(j + 1) * P], ident[:, :])
            last.then_inc(wxt_t, 1)
            pe.wait_ge(wxt_c, 2)
            wx4 = wxt.rearrange("p a b -> p (a b)").rearrange("p (c j n) -> p c j n", c=CT, j=KT)
            for h in (*range(0, H, 2), *range(1, H, 2)):
                u = (h % 2) * D
                if h == 1:
                    pe.wait_ge(pe_step, 1)
                for ct in range(CT):
                    pe.matmul(ps[:, HA + ct, h * G:(h + 1) * G], wx4[u:u + D, ct, h // 2, :], wsl[u:u + D, :],
                              start=True, stop=True)
                last = pe.matmul(ps[:, XA, h * G:(h + 1) * G], bxb[u:u + D, h // 2, :], wsl[u:u + D, :],
                                 start=True, stop=True)
                if h == H - 2:
                    last.then_inc(pe_step, 1)
            last.then_inc(wxs_m, 1)
            pe.wait_ge(plan_cnt, 1)
            pe.transpose(ps[0:1, 1, 64:64 + NW + 1], col[0:NW + 1, 3:4], ident[0:NW + 1, 0:NW + 1]).then_inc(plan_t, 1)
            pe.wait_ge(plan_done, 2)
            general = pe.value_load(flag_i[0:1, 0:1], min_val=0, max_val=1)
            with pe.If(general):
                pe.sem_inc(gen_mm, 1)
                with pe.Fori(0, NW) as w:
                    pe.wait_ge(gen_sum, w + 1)
                    pe.matmul(ps[:, SUM_A, :], zeros[:, 0:P], zeros, start=True, stop=False)
                    with pe.Fori(0, ROUNDS) as r:
                        n = w * ROUNDS + r
                        pe.wait_ge(gen_hot, n + 1)
                        pe.wait_ge(gen_rows, n * (16 * CH) + 16 * CH)
                        for j in range(CH):
                            last = pe.matmul(ps[0:WN, SUM_A, :], oneh[:, 0, j, 0:WN], ring[:, 0, j, :],
                                             start=False, stop=False, skip_group_check=True)
                        last.then_inc(gen_mm, 1)
                    pe.matmul(ps[:, SUM_A, :], zeros[:, 0:P], zeros, start=False, stop=True).then_inc(gen_zero, 1)

            for n in range(MT):
                s = n % (MT // 2)
                pe.wait_ge(ld_wih, 16 * (MT // 2) * (1 + n // (MT // 2)))
                if n < 2:
                    pe.wait_ge(wxs_c, 3)
                else:
                    pe.wait_ge(wprep_h, n)
                    pe.wait_ge(wprep_l, n)
                for k in range(KT):
                    last = pe.transpose(ps[:, XA + n % 2, k * P:(k + 1) * P], raw[:, s * HID + k * P:s * HID + (k + 1) * P],
                                        ident[:, :])
                last.then_inc(wprep_t, 1)

            def sums_of(p, e):
                pe.wait_ge(hot_done[e], p + 1)
                for j in range(CH):
                    if j % HALF == 0:
                        pe.wait_ge(rows_in[e][j // HALF], 16 * HALF * p + 16 * HALF)
                    last = pe.matmul(ps[0:WN, SUM_A + e, :], oneh[:, e, j, 0:WN], ring[:, e, j, :],
                                     start=(j == 0), stop=(j == CH - 1))
                    if j == HALF - 1:
                        last.then_inc(half_used[e], 1)
                last.then_inc(sum_done[e], 1)

            def transpose_x(p, swt_before):
                for e in range(2):
                    pe.wait_ge(agg_done[e], p + 1)
                pe.wait_ge(xn_in, 32 * p + 32)
                if swt_before is not None:
                    after(pe, swt_done, swt_before)
                for e in range(2):
                    for q in range(2):
                        for hh in range(CT):
                            pe.transpose(xx16[:, hh, q, e * P:e * P + WN],
                                         xn16[0:WN, e, q * C + hh * P:q * C + (hh + 1) * P], ident16[0:WN, 0:WN])
                    for hh in range(CT):
                        last = pe.transpose(ps[:, XA, hh * 256 + e * P:hh * 256 + e * P + WN],
                                            agg[0:WN, e, hh * P:(hh + 1) * P], ident[0:WN, 0:WN])
                last.then_inc(xt_done, 1)

            def graph_layer(p):
                pe.wait_ge(xsplit_a, 5 * p + 5)
                pe.wait_ge(xsplit_v, p + 1)
                after(pe, gate_act, MT * p)
                for m in range(KT):
                    dst = ps[:, HA + m // 2, (m % 2) * 256:(m % 2) * 256 + 256]
                    for k in range(2 * CT):
                        xh, xl = ((at_h, at_l), (xt_h, xt_l))[k // CT]
                        last = three(pe, dst, w1_h[:, k, m * P:(m + 1) * P], w1_l[:, k, m * P:(m + 1) * P],
                                     xh[:, k % CT, :], xl[:, k % CT, :], k == 0, k == 2 * CT - 1)
                    if m % 2:
                        last.then_inc(h_mm, 1)

            def transpose_x2(p):
                pe.wait_ge(x2_norm, 2 * p + 2)
                for e in range(2):
                    for hh in range(CT):
                        last = pe.transpose(ps[:, XX, hh * 256 + e * P:hh * 256 + e * P + WN],
                                            x2[0:WN, e, hh * P:(hh + 1) * P], ident[0:WN, 0:WN])
                last.then_inc(x2t_mm, 1)

            def logits(p):
                pe.wait_ge(x2t_hi, p + 1)
                pe.wait_ge(x2t_lo, p + 1)
                for e in range(2):
                    for hh in range(CT):
                        dst = ps[0:WN, XA + e, :]
                        c = slice(e * P, e * P + WN)
                        last = three(pe, dst, x2t_h[:, hh, c], x2t_l[:, hh, c], wxs_h[:, hh, :], wxs_l[:, hh, :],
                                     hh == 0, hh == CT - 1)
                    last.then_inc(lg_mm, 1)

            def cell_gates(p, n0, n1):
                if n0 == 0:
                    pe.wait_ge(h_hi, 2 * p + 2)
                    pe.wait_ge(h_lo, 2 * p + 2)
                for n in range(n0, n1):
                    s = n % 4
                    if n >= 4 and n % 2 == 0:
                        pe.wait_ge(gate_act, MT * p + n - 2)
                    dst = ps[:, HA + s // 2, (s % 2) * 256:(s % 2) * 256 + 256]
                    for k in range(KT):
                        last = three(pe, dst, wih_h[:, k, n, :], wih_l[:, k, n, :], h_h[:, k, :], h_l[:, k, :],
                                     k == 0, k == KT - 1)
                    if n % 2:
                        last.then_inc(gate_mm, 1)

            def token_sums(p):
                pe.wait_ge(sw_done, p + 1)
                for e in range(2):
                    for j in range(KT):
                        last = pe.transpose(ps[:, XA + e, j * P:j * P + WN], sw[0:WN, e, j * P:(j + 1) * P], ident[0:WN, 0:WN])
                    last.then_inc(swt_mm, 1)
                pe.wait_ge(x2_hi, p + 1)
                pe.wait_ge(x2_lo, p + 1)
                pe.wait_ge(sw_hi, p + 1)
                pe.wait_ge(sw_lo, p + 1)
                for hh in range(CT):
                    for e in range(2):
                        c = slice(hh * P, (hh + 1) * P)
                        for i, (wx, s) in enumerate(((x2_h, sw_h), (x2_h, sw_l), (x2_l, sw_h))):
                            end = isinstance(p, int) and p == NP - 1 and e == 1 and i == 2
                            last = pe.matmul(ps[:, TOK + hh, :], wx[0:WN, e, c], s[0:WN, e, :], start=False, stop=end,
                                             skip_group_check=not end)
                last.then_inc(tok_mm, 1)

            def out_layer(p, sums_before):
                pe.wait_ge(hl_hi, 2 * p + 2)
                pe.wait_ge(hl_lo, 2 * p + 2)
                pe.wait_ge(agg_done[1], sums_before)
                for e in range(2):
                    for k in range(KT):
                        c = slice(e * P, e * P + WN)
                        last = three(pe, ps[0:WN, SUM_B, e * C:(e + 1) * C], hl_h[:, k, c], hl_l[:, k, c],
                                     wfc_h[:, k, :], wfc_l[:, k, :], k == 0, k == KT - 1)
                last.then_inc(y_mm, 1)

            def turn(t, gather, gnn, ffn, ahead):
                if gnn:
                    transpose_x(t - 1, 2 * (t - 2) if ffn else None)
                if gather:
                    sums_of(t, 0)
                if ffn:
                    out_layer(t - 2, t if gnn else NP)
                if gnn:
                    graph_layer(t - 1)
                if gather:
                    if ffn:
                        pe.wait_ge(x2_step, 4 * (t - 2) + 1)
                    sums_of(t, 1)
                if ffn:
                    transpose_x2(t - 2)
                if gnn:
                    if isinstance(t, int) and t == 1:
                        pe.wait_ge(wprep_h, MT + 2)
                        pe.wait_ge(wprep_l, MT + 2)
                    cell_gates(t - 1, 0, 4)
                if ffn:
                    logits(t - 2)
                if gnn:
                    cell_gates(t - 1, 4, MT)
                if ffn:
                    token_sums(t - 2)

            lo, hi = turns(turn)
            with pe.Fori(lo, hi) as t:
                turn(t, True, True, True, True)
            last_turns(turn)

            pe.wait_ge(norm_add, 2 * NP)
            for h in range(H):
                last = pe.matmul(ps[0:G, 0, h:h + 1], norm[0:WN, h * G:(h + 1) * G], ones[0:WN, 0:1], start=True, stop=True)
            last.then_inc(att_pe, 1)
            pe.wait_ge(ld_att, 16 * 6)
            pe.wait_ge(att_v, V_TKS)
            for h in range(H):
                c = slice(h * G, (h + 1) * G)
                for ct in range(CT):
                    last = pe.matmul(ps[0:G, 1, c], tks[:, ct, c], wfx[:, ct, c], start=(ct == 0), stop=(ct == CT - 1))
            last.then_inc(att_pe, 1)
            pe.wait_ge(att_v, V_TOKENS)
            for h in range(H):
                c = slice(h * G, (h + 1) * G)
                last = pe.transpose(ps[0:G, 2, c], tokens[:, c], ident[0:G, 0:G])
            last.then_inc(att_pe, 1)
            pe.wait_ge(att_v, V_TOKT)
            pe.matmul(ps[0:D, 3, :], wqkv[:, 0, :], tokt[:, :], start=True, stop=True)
            pe.matmul(ps[0:D, 4, :], wqkv[:, 1, :], tokt[:, :], start=True, stop=True)
            for h in range(H):
                c = slice(h * G, (h + 1) * G)
                last = pe.matmul(ps[0:G, 5, c], tokt[:, c], wqkv[:, 2, :], start=True, stop=True)
            last.then_inc(att_pe, 1)
            pe.wait_ge(att_v, V_QKV)
            for h in range(H):
                c = slice(h * G, (h + 1) * G)
                last = pe.matmul(ps[0:G, 0, c], qt[:, c], kt[:, c], start=True, stop=True)
            last.then_inc(att_pe, 1)
            pe.wait_ge(att_v, V_ATT)
            for h in range(H):
                c = slice(h * G, (h + 1) * G)
                last = pe.transpose(ps[0:G, 1, c], att[:, c], ident[0:G, 0:G])
            last.then_inc(att_pe, 1)
            pe.wait_ge(att_v, V_ATTT)
            for h in range(H):
                c = slice(h * G, (h + 1) * G)
                last = pe.matmul(ps[0:D, 2, c], vv[:, c], attt[:, c], start=True, stop=True)
            last.then_inc(att_pe, 1)
            pe.wait_ge(att_v, V_OST)
            for h in range(H):
                u, j = (h % 2) * G, h // 2
                last = pe.matmul(ps[u:u + G, 3 + j // 2, (j % 2) * C:(j % 2) * C + C], ost[:, h * G:(h + 1) * G],
                                 wout[:, h, :], start=True, stop=True, skip_group_check=True)
            last.then_inc(att_pe, 1)
            pe.wait_ge(att_a, 3)
            pe.wait_ge(att_v, V_VLO)

            for k in range(2):
                pe.sem_inc(f_mm[k], 1)

            def f_mul(n, k):
                pe.wait_ge(f_hi[k], n + 1)
                pe.wait_ge(f_lo[k], n + 1)
                pe.wait_ge(f_out[k], n + 1)
                sh, sl = (x[k].rearrange("p (e j n) -> p e j n", e=2, j=KT) for x in (fsw_h, fsw_l))
                for e in range(2):
                    for j in range(KT):
                        last = three(pe, ps[0:WN, TOK + k, e * C:(e + 1) * C], sh[:, e, j, :], sl[:, e, j, :],
                                     v_h[:, j, :], v_l[:, j, :], j == 0, j == KT - 1)
                last.then_inc(f_mm[k], 1)

            with pe.Fori(0, NP // 2) as n:
                f_mul(n, 0)
                f_mul(n, 1)
            f_mul(NP // 2, 0)

        @block.vector
        def _(dve):
            steps = [0]

            def link(ins):
                steps[0] += 1
                ins.then_inc(dve_step, 1)
                dve.wait_ge(dve_step, steps[0])

            dve.wait_ge(consts, NCONST)
            dve.tensor_copy(ident16[:, :], ident[:, :]).then_inc(w_ready, 1)

            def ln_stats(k):
                n, rows = (P, LR) if k < NCH else (REST, 1)
                q = k % 2
                dve.wait_ge(ln_in[k % 3], 16 * (k // 3 + 1))
                for r in range(rows):
                    steps[0] += 1
                    dve.bn_stats(stats[0:n, q, r, :], lx[k % 3][0:n, r, :]).then_inc(dve_step, 1)
                dve.wait_ge(dve_step, steps[0])
                for r in range(rows):
                    last = dve.bn_aggr(mv[0:n, q, r, :], stats[0:n, q, r, :])
                last.then_inc(ln_var, 1)

            def ln_scale(k):
                n, rows = (P, LR) if k < NCH else (REST, 1)
                q = k % 2
                dve.wait_ge(ln_sd, k + 1)
                link(dve.reciprocal(rstd[0:n, q, 0:rows], sd[0:n, q, 0:rows]))
                dve.scalar_tensor_tensor(out=nmr[0:n, q, 0:rows], in0=mv[0:n, q, 0:rows, 0], scalar=-1.0,
                                         in1=rstd[0:n, q, 0:rows], op0=ALU.mult, op1=ALU.mult).then_inc(ln_rstd, 1)

            def ln_low(k):
                n, rows = (P, LR) if k < NCH else (REST, 1)
                q = k % 2
                dve.wait_ge(ln_x, min(LR * (k + 1), LR * NCH + 1))
                dve.wait_ge(ln_hi, k + 1)
                dve.tensor_tensor(lt[q][0:n, 0:rows, C:2 * C], ln[q][0:n, 0:rows, :], lt[q][0:n, 0:rows, 0:C],
                                  ALU.subtract).then_inc(ln_lo, 1)

            def plan_a():
                dve.wait_ge(ld_tab, 32)
                link(dve.tensor_copy(edge_f[0:WN, :], edge_i[0:WN, :]))
                dve.tensor_scalar(pick[0:WN, 0:NW + 1], wbase[0:WN, 0:NW + 1], edge_f[0:WN, 0:1], None,
                                  ALU.is_gt).then_inc(plan_m, 1)
                link(dve.tensor_tensor(edge_le[0:WN, :], edge_f[0:WN, 0:ER], edge_f[0:WN, 1:ER + 1], ALU.is_le))
                dve.tensor_reduce(col[0:WN, 0:1], edge_le[0:WN, :], AX.X, ALU.add).then_inc(plan_m, 1)

            def plan_b():
                dve.wait_ge(plan_pw, 1)
                link(dve.tensor_scalar(col[0:NW + 1, 1:2], ps[0:NW + 1, 0, 0:1], 1.0, 0.0, ALU.subtract, ALU.max))
                dve.tensor_copy(coli[0:NW + 1, :], col[0:NW + 1, 1:2]).then_inc(plan_row, 1)

            def plan_c():
                dve.wait_ge(ld_rows, 16)
                link(dve.tensor_copy(edge_f[0:NW + 1, 0:ER], edge_i[0:NW + 1, 0:ER]))
                link(dve.tensor_scalar(edge_le[0:NW + 1, :], edge_f[0:NW + 1, 0:ER], col[0:NW + 1, 7:8], None, ALU.is_lt))
                link(dve.tensor_reduce(col[0:NW + 1, 2:3], edge_le[0:NW + 1, :], AX.X, ALU.add))
                dve.scalar_tensor_tensor(out=col[0:NW + 1, 3:4], in0=col[0:NW + 1, 1:2], scalar=float(ER),
                                         in1=col[0:NW + 1, 2:3], op0=ALU.mult, op1=ALU.add).then_inc(plan_cnt, 1)

            def plan_d():
                dve.wait_ge(plan_t, 1)
                link(dve.tensor_copy(row[:, 0, 0:NW + 1], ps[0:1, 1, 64:64 + NW + 1]))
                link(dve.tensor_tensor(row[:, 1, 0:NW], row[:, 0, 1:NW + 1], row[:, 0, 0:NW], ALU.subtract))
                link(dve.tensor_reduce(row[:, 2, 0:1], row[:, 1, 0:NW], AX.X, ALU.max))
                link(dve.tensor_scalar(row[:, 2, 1:2], row[:, 2, 0:1], float(CAP), None, ALU.is_gt))
                link(dve.tensor_scalar(row[:, 2, 2:3], ps[0:1, 1, 0:1], float(E), None, ALU.is_lt))
                link(dve.tensor_tensor(row[:, 2, 3:4], row[:, 2, 1:2], row[:, 2, 2:3], ALU.max))
                dve.tensor_copy(flag_i[:, :], row[:, 2, 3:4]).then_inc(plan_done, 1)
                link(dve.tensor_scalar(row[:, 3, 0:NW], row[:, 0, 0:NW], -1.0, float(E), ALU.mult, ALU.add))
                link(dve.tensor_scalar(row[:, 4, 0:NW], row[:, 3, 0:NW], row[:, 2, 3:4], None, ALU.mult))
                dve.tensor_tensor(base_i[:, 0:NW], row[:, 0, 0:NW], row[:, 4, 0:NW], ALU.add).then_inc(plan_done, 1)

            def bias_rows():
                dve.wait_ge(ld_small, 16 * (1 + 6 + 1 + 3 + 1 + 2))
                link(dve.tensor_scalar(rtemp[:, :], temp8[:, :], 0.1, 5.0, ALU.max, ALU.min))
                link(dve.reciprocal(rtemp[:, :], rtemp[:, :]))
                for g in range(3):
                    link(dve.tensor_tensor(bgate[:, :, g], braw[:, 0, g, :], braw[:, 1, g, :], ALU.add))
                for g in (0, 2):
                    link(dve.tensor_scalar(bgate[:, :, g], bgate[:, :, g], 0.5, None, ALU.mult))
                link(dve.tensor_copy(bxb, bxc.unsqueeze(2).to_broadcast([P, KT, P])))
                dve.wait_ge(wxt_t, 1)
                wx4 = wxt.rearrange("p a b -> p (a b)").rearrange("p (c n) -> p c n", c=CT)
                dve.tensor_copy(wx4, ps[:, XA:XA + 2, :]).then_inc(wxt_c, 2)

            def slice_weights():
                dve.wait_ge(wxs_m, 1)
                for ct in range(CT):
                    dve.tensor_tensor(sw[:, ct, :].rearrange("p (h g) -> p h g", g=G),
                                      ps[:, HA + ct, :].rearrange("p (h g) -> p h g", g=G),
                                      rtemp[:, :].unsqueeze(2).to_broadcast([P, H, G]), ALU.mult).then_inc(wxs_c, 1)
                b3 = biasx[:, :].rearrange("p (h g) -> p h g", g=G)
                link(dve.tensor_tensor(b3, ps[:, XA, :].rearrange("p (h g) -> p h g", g=G),
                                       bsl.unsqueeze(1).to_broadcast([P, H, G]), ALU.add))
                dve.tensor_tensor(b3, b3, rtemp[:, :].unsqueeze(2).to_broadcast([P, H, G]), ALU.mult).then_inc(wxs_c, 1)
                dve.wait_ge(wprep_h, 1)
                dve.wait_ge(wxs_c, 2)
                dve.tensor_tensor(wxs_l[:, :, :], sw[:, :, :], wxs_h[:, :, :].bitcast(F32), ALU.subtract).then_inc(wprep_l, 1)

            ln_stats(0)
            for k in range(NCH + 1):
                ln_scale(k)
                if k < NCH:
                    ln_stats(k + 1)
                if k >= 1:
                    ln_low(k - 1)
                if k == 1:
                    plan_a()
                if k == 3:
                    plan_b()
                if k == 6:
                    bias_rows()
                if k == 8:
                    plan_c()
                if k == 10:
                    plan_d()
            ln_low(NCH)
            general = dve.value_load(flag_i[0:1, 0:1], min_val=0, max_val=1)

            def one_hots(e, base, rel_sem, rel_n, hot_sem):
                dve.tensor_scalar(rel[:, e, :], didx[:, e, :], base, None, ALU.subtract).then_inc(rel_sem, 1)
                dve.wait_ge(rel_sem, rel_n)
                for j in range(CH):
                    last = dve.tensor_scalar(oneh[:, e, j, 0:WN], iota[:, 0:WN], rel[:, e, j:j + 1], None, ALU.is_equal)
                last.then_inc(hot_sem, 1)

            with dve.If(general):
                dve.sem_inc(gen_sum, 1)
                with dve.Fori(0, NW) as w:
                    with dve.Fori(0, ROUNDS) as r:
                        n = w * ROUNDS + r
                        dve.wait_ge(gen_idx, n * 32 + 32)
                        dve.wait_ge(gen_mm, n + 1)
                        one_hots(0, wbase[:, ds(w, 1)], gen_rel, n + 1, gen_hot)
                    dve.wait_ge(gen_zero, w + 1)
                    dve.wait_ge(gen_st, w * 16 + 16)
                    dve.tensor_copy(agg[0:WN, 1, :], ps[0:WN, SUM_A, 0:C]).then_inc(gen_rel2, 1)
                    dve.wait_ge(gen_rel2, w + 1)
                    dve.tensor_tensor(agg[0:WN, 0, :], agg[0:WN, 1, :], ps[0:WN, SUM_A, C:2 * C], ALU.add).then_inc(gen_sum, 1)

            def hots(p, e):
                dve.wait_ge(idx_in[e], 32 * p + 32)
                after(dve, sum_done[e], p)
                one_hots(e, wbase[:, ds(2 * p + e, 1)], rel_done[e], p + 1, hot_done[e])

            def add_halves(p, e):
                dve.wait_ge(sum_done[e], p + 1)
                after(dve, xt_done, p)
                dve.tensor_copy(agg[0:WN, e, :], ps[0:WN, SUM_A + e, C:2 * C]).then_inc(low_out[e], 1)
                with dve.If(general):
                    dve.wait_ge(gen_in, 32 * p + 32)
                    dve.wait_ge(low_out[e], p + 1)
                    dve.tensor_tensor(agg[0:WN, e, :], agg[0:WN, e, :], extra[0:WN, e, :], ALU.add).then_inc(gen_add, 1)
                    dve.wait_ge(gen_add, 2 * p + e + 1)
                    dve.tensor_tensor(agg[0:WN, e, :], agg[0:WN, e, :], ps[0:WN, SUM_A + e, 0:C],
                                      ALU.add).then_inc(agg_done[e], 1)
                with dve.Else():
                    dve.wait_ge(low_out[e], p + 1)
                    dve.tensor_tensor(agg[0:WN, e, :], agg[0:WN, e, :], ps[0:WN, SUM_A + e, 0:C],
                                      ALU.add).then_inc(agg_done[e], 1)

            def split_x(p):
                dve.wait_ge(xsplit_a, 5 * p + 1)
                dve.tensor_tensor(valid(at_l[:, :, :]), bank_valid(XA), valid(at_h[:, :, :]).bitcast(F32),
                                  ALU.subtract).then_inc(xsplit_v, 1)

            def norm_x2(p):
                dve.wait_ge(y_mm, p + 1)
                dve.wait_ge(x_in, 32 * p + 32)
                after(dve, x2t_mm, p)
                after(dve, x2_hi, p)
                y = ps[0:WN, SUM_B, :].rearrange("p (e c) -> p e c", e=2)
                dve.tensor_tensor(x2[0:WN, :, :], y, xin[0:WN, :, :], ALU.add).then_inc(x2_step, 1)
                dve.wait_ge(x2_step, 4 * p + 1)
                dve.tensor_tensor(x2[0:WN, :, :], x2[0:WN, :, :], bfc[0:WN, :].unsqueeze(1).to_broadcast([WN, 2, C]),
                                  ALU.add).then_inc(x2_step, 1)
                dve.wait_ge(x2_step, 4 * p + 2)
                for e in range(2):
                    dve.bn_stats(stats[0:WN, 0, e, :], x2[0:WN, e, :]).then_inc(x2_step, 1)
                dve.wait_ge(x2_step, 4 * p + 4)
                dve.tensor_tensor(xin[0:WN, :, :], x2[0:WN, :, :], bout[0:WN, :].unsqueeze(1).to_broadcast([WN, 2, C]),
                                  ALU.add).then_inc(res_done, 1)
                for e in range(2):
                    dve.bn_aggr(mv[0:WN, 0, e, :], stats[0:WN, 0, e, :]).then_inc(var_done, 1)
                dve.wait_ge(sd_done, p + 1)
                dve.reciprocal(rstd[0:WN, 0, 0:2], sd[0:WN, 0, 0:2]).then_inc(rstd_done, 1)
                dve.wait_ge(rstd_done, 2 * p + 1)
                dve.scalar_tensor_tensor(out=nmr[0:WN, 0, 0:2], in0=mv[0:WN, 0, 0:2, 0], scalar=-1.0,
                                         in1=rstd[0:WN, 0, 0:2], op0=ALU.mult, op1=ALU.mult).then_inc(rstd_done, 1)

            def low_x2(p):
                dve.wait_ge(x2_hi, p + 1)
                after(dve, tok_mm, p)
                dve.tensor_tensor(x2_l[0:WN, :, :], x2[0:WN, :, :], x2_h[0:WN, :, :].bitcast(F32),
                                  ALU.subtract).then_inc(x2_lo, 1)

            def low_h(p, q):
                dve.wait_ge(h_hi, 2 * p + q + 1)
                dve.tensor_tensor(h_l[:, 2 * q:2 * q + 2, :], hf[:, 2 * q:2 * q + 2, :],
                                  h_h[:, 2 * q:2 * q + 2, :].bitcast(F32), ALU.subtract).then_inc(h_lo, 1)

            def low_x2t(p):
                dve.wait_ge(x2t_hi, p + 1)
                dve.tensor_tensor(valid(x2t_l[:, :, :]), bank_valid(XX), valid(x2t_h[:, :, :]).bitcast(F32),
                                  ALU.subtract).then_inc(x2t_lo, 1)

            def heads(x):
                return x[0:WN, :, :].rearrange("p e (h g) -> p (e h) g", g=G)

            def softmax(p):
                dve.wait_ge(lg_mm, 2 * p + 2)
                after(dve, swt_mm, 2 * p)
                after(dve, sw_hi, p)
                dve.tensor_tensor(sw[0:WN, :, :], ps[0:WN, XA:XA + 2, :],
                                  biasx[0:WN, :].unsqueeze(1).to_broadcast([WN, 2, HG]), ALU.add).then_inc(sm_step, 1)
                dve.wait_ge(sm_step, 4 * p + 1)
                dve.tensor_reduce(mx8[0:WN, :], heads(sw), AX.X, ALU.max).then_inc(sm_step, 1)
                dve.wait_ge(sm_step, 4 * p + 2)
                dve.tensor_tensor(heads(sw), heads(sw), mx8[0:WN, :].unsqueeze(2).to_broadcast([WN, 2 * H, G]),
                                  ALU.subtract).then_inc(lg_sub, 1)

            def softmax_end(p):
                dve.wait_ge(lg_exp, p + 1)
                dve.tensor_reduce(sm8[0:WN, :], heads(sw), AX.X, ALU.add).then_inc(sm_step, 1)
                dve.wait_ge(sm_step, 4 * p + 3)
                dve.reciprocal(rs8[0:WN, :], sm8[0:WN, :]).then_inc(sm_step, 1)
                dve.wait_ge(sm_step, 4 * p + 4)
                dve.tensor_tensor(heads(sw), heads(sw), rs8[0:WN, :].unsqueeze(2).to_broadcast([WN, 2 * H, G]),
                                  ALU.mult).then_inc(sw_done, 1)
                dve.wait_ge(sw_done, p + 1)
                for e in range(2):
                    after(dve, norm_add, 2 * p + e)
                    dve.tensor_tensor(norm[0:WN, :], norm[0:WN, :], sw[0:WN, e, :], ALU.add).then_inc(norm_add, 1)

            def low_sw(p):
                dve.wait_ge(sw_hi, p + 1)
                after(dve, tok_mm, p)
                dve.tensor_tensor(sw_l[0:WN, :, :], sw[0:WN, :, :], sw_h[0:WN, :, :].bitcast(F32),
                                  ALU.subtract).then_inc(sw_lo, 1)

            def cell_c(p, f):
                dve.wait_ge(gate_act, MT * p + 3 * f + 3)
                dve.scalar_tensor_tensor(out=gate[:, 0, f, :], in0=gate[:, 0, f, :], scalar=1.0, in1=gate[:, 1, f, :],
                                         op0=ALU.add, op1=ALU.mult).then_inc(cell_v, 1)

            def cell_o(p, f):
                dve.wait_ge(cell_t, KT * p + f + 1)
                dve.scalar_tensor_tensor(out=hf[:, f, :], in0=gate[:, 2, f, :], scalar=1.0, in1=gate[:, 1, f, :],
                                         op0=ALU.add, op1=ALU.mult).then_inc(cell_out, 1)

            def low_hl(p, q):
                if q == 0:
                    after(dve, y_mm, p)
                dve.wait_ge(hl_hi, 2 * p + q + 1)
                dve.tensor_tensor(hl_l[:, 2 * q:2 * q + 2, :], hf[:, 2 * q:2 * q + 2, :],
                                  hl_h[:, 2 * q:2 * q + 2, :].bitcast(F32), ALU.subtract).then_inc(hl_lo, 1)

            def turn(t, gather, gnn, ffn, ahead):
                if gnn:
                    split_x(t - 1)
                if gather:
                    add_halves(t, 0)
                if ahead:
                    hots(t + 1, 0)
                if ffn:
                    norm_x2(t - 2)
                if gnn:
                    low_h(t - 1, 0)
                    low_h(t - 1, 1)
                if ffn:
                    low_x2(t - 2)
                if gather:
                    add_halves(t, 1)
                if ffn:
                    low_x2t(t - 2)
                if ahead:
                    hots(t + 1, 1)
                if gnn:
                    cell_c(t - 1, 0)
                    cell_o(t - 1, 0)
                if ffn:
                    softmax(t - 2)
                if gnn:
                    cell_c(t - 1, 1)
                    cell_o(t - 1, 1)
                if ffn:
                    softmax_end(t - 2)
                    low_sw(t - 2)
                if gnn:
                    cell_c(t - 1, 2)
                    cell_o(t - 1, 2)
                    cell_c(t - 1, 3)
                    cell_o(t - 1, 3)
                    low_hl(t - 1, 0)
                    low_hl(t - 1, 1)

            hots(0, 0)
            hots(0, 1)
            dve.wait_ge(w1_free, 1)
            dve.tensor_tensor(w1_l[:, :, :], raw[:, 0:4 * HID].rearrange("p (k n) -> p k n", n=HID),
                              w1_h[:, :, :].bitcast(F32), ALU.subtract).then_inc(w1_free, 1)
            slice_weights()
            for n in range(MT):
                dve.wait_ge(wprep_h, n + 2)
                dve.tensor_tensor(wih_l[:, :, n, :], ps[:, XA + n % 2, :].rearrange("p (k m) -> p k m", m=P),
                                  wih_h[:, :, n, :].bitcast(F32), ALU.subtract).then_inc(wprep_l, 1)
            dve.wait_ge(wprep_h, MT + 2)
            dve.scalar_tensor_tensor(out=wfc_l[:, :, :], in0=raw[:, 0:KT * C].rearrange("p (k n) -> p k n", n=C),
                                     scalar=0.5, in1=wfc_h[:, :, :].bitcast(F32), op0=ALU.mult,
                                     op1=ALU.subtract).then_inc(wprep_l, 1)
            lo, hi = turns(turn)
            with dve.Fori(lo, hi) as t:
                turn(t, True, True, True, True)
            last_turns(turn)

            count = [0]

            def step(ins, wait=True):
                count[0] += 1
                ins.then_inc(att_v, 1)
                if wait:
                    dve.wait_ge(att_v, count[0])

            def hd(x):
                return x.rearrange("p (h g) -> p h g", h=H)

            def spread(x):
                return x.unsqueeze(2).to_broadcast([G, H, D])

            dve.wait_ge(tok_mm, NP)
            dve.wait_ge(sum_done[1], NP)
            step(dve.tensor_copy(tks, ps[:, TOK:TOK + 2, :]))
            assert count[0] == V_TKS
            dve.wait_ge(att_pe, 1)
            nc8, rn8, nr8 = mx8[0:G, 0:H], rs8[0:G, 0:H], sm8[0:G, 0:H]
            step(dve.tensor_scalar(nc8, ps[0:G, 0, 0:H], 1e-5, None, ALU.add))
            step(dve.reciprocal(rn8, nc8))
            step(dve.tensor_tensor(nr8, ps[0:G, 0, 0:H], rn8, ALU.mult))
            dve.wait_ge(ld_att, 16 * 6)
            step(dve.tensor_tensor(hd(tmp), hd(bfx), spread(nr8), ALU.mult))
            dve.wait_ge(att_pe, 2)
            step(dve.tensor_tensor(hd(tokens), hd(ps[0:G, 1, :]), spread(rn8), ALU.mult))
            step(dve.tensor_tensor(tokens, tokens, tmp, ALU.add))
            assert count[0] == V_TOKENS
            dve.wait_ge(att_pe, 3)
            step(dve.tensor_copy(tokt, ps[0:G, 2, :]))
            assert count[0] == V_TOKT
            dve.wait_ge(att_pe, 4)
            for x, b in ((qt, 3), (kt, 4), (vv, 5)):
                step(dve.tensor_copy(x, ps[0:G, b, :]), False)
            assert count[0] == V_QKV
            dve.wait_ge(att_pe, 5)
            step(dve.tensor_reduce(mx8[0:G, 0:H], hd(ps[0:G, 0, :]), AX.X, ALU.max))
            step(dve.tensor_tensor(hd(att), hd(ps[0:G, 0, :]), spread(mx8[0:G, 0:H]), ALU.subtract))
            assert count[0] == ATT_SUB
            dve.wait_ge(att_a, 1)
            step(dve.tensor_reduce(sm8[0:G, 0:H], hd(att), AX.X, ALU.add))
            step(dve.reciprocal(rs8[0:G, 0:H], sm8[0:G, 0:H]))
            step(dve.tensor_tensor(hd(att), hd(att), spread(rs8[0:G, 0:H]), ALU.mult))
            assert count[0] == V_ATT
            dve.wait_ge(att_pe, 6)
            step(dve.tensor_copy(attt, ps[0:G, 1, :]))
            assert count[0] == V_ATTT
            dve.wait_ge(att_pe, 7)
            step(dve.tensor_copy(ost, ps[0:G, 2, :]))
            assert count[0] == V_OST
            for b in range(2):
                dve.wait_ge(att_a, 2 + b)
                step(dve.tensor_tensor(v_l[:, 2 * b:2 * b + 2, :], ps[:, 3 + b, :].rearrange("p (j c) -> p j c", c=C),
                                       v_h[:, 2 * b:2 * b + 2, :].bitcast(F32), ALU.subtract), False)
            assert count[0] == V_VLO

            def f_low(n, k):
                dve.wait_ge(f_hi[k], n + 1)
                dve.tensor_tensor(fsw_l[k], fsw[k], fsw_h[k].bitcast(F32), ALU.subtract).then_inc(f_lo[k], 1)

            def f_add(n, k):
                dve.wait_ge(f_mm[k], n + 2)
                dve.wait_ge(f_res[k], 32 * n + 32)
                after(dve, f_st[k], 32 * n)
                dve.tensor_tensor(fo[0:WN, k, :], ps[0:WN, TOK + k, :],
                                  fres[0:WN, k, :, :].rearrange("p e c -> p (e c)"), ALU.add).then_inc(f_out[k], 1)

            for k in range(2):
                dve.sem_inc(f_out[k], 1)
            f_low(0, 0)

            def f_both(n):
                f_low(n, 1)
                f_add(n, 0)
                f_low(n + 1, 0)
                f_add(n, 1)

            f_both(0)
            with dve.Fori(1, NP // 2) as n:
                f_both(n)
            f_add(NP // 2, 0)


_INS = ["x", "src", "dst", "W_rel", "b_rel", "W_root", "W_ih", "b_ih", "b_hh", "W_fc", "b_fc",
        "W_fx", "b_fx", "W_x", "b_x", "W_slice", "b_slice", "W_q", "W_k", "W_v", "W_out", "b_out", "temperature"]
_GNN = ("W_rel", "b_rel", "W_root", "W_ih", "b_ih", "b_hh", "W_fc", "b_fc")


def kernel(**inputs):
    import numpy as np
    from concourse import bacc
    from concourse.bass_utils import run_bass_kernel_spmd

    nc = bacc.Bacc("TRN2", target_bir_lowering=False, num_devices=1)
    arrays, args = {}, {}
    for name in _INS:
        full = name if name in ("x", "src", "dst") else ("L0_gnn_" if name in _GNN else "L0_ffn_") + name
        v = np.ascontiguousarray(inputs[full])
        arrays[f"in_{name}"] = v
        args[name] = nc.dram_tensor(f"in_{name}", v.shape, mybir.dt.from_np(v.dtype), kind="ExternalInput").ap()
    out = nc.dram_tensor("out_x", inputs["x"].shape, F32, kind="ExternalOutput").ap()
    build_program(nc, args, out)
    r = run_bass_kernel_spmd(nc, [arrays], core_ids=[0])
    return r.results[0]["out_x"]
```

```python
from contextlib import ExitStack

import concourse.bass as bass
from concourse import mybir

F32 = mybir.dt.float32
F32R = mybir.dt.float32r
F16 = mybir.dt.float16
I32 = mybir.dt.int32
ALU = mybir.AluOpType
ACT = mybir.ActivationFunctionType
AX = mybir.AxisListType
ds = bass.ds

P = 128
EPS = 1e-5


def build_program(nc, a, out):
    N, C = a["x"].shape
    (E,) = a["src"].shape
    HID = a["W_rel"].shape[1]
    G = a["W_slice"].shape[1]
    D = a["W_slice"].shape[0]
    H = a["temperature"].shape[1]
    HG = H * G
    WN = 125
    NW = N // WN
    NP = NW // 2
    CH = 18
    HALF = CH // 2
    CAP = CH * P
    ROUNDS = -(-E // CAP)
    GW = 5
    NG = NW // GW
    EP = max(E + CAP, ROUNDS * CAP)
    ER = E // WN
    NOWHERE = 8191
    KT = HID // P
    CT = C // P
    GATES = (0, 2, 3)
    MT = 3 * KT
    SCALE = float(D) ** -0.5
    FB = 4
    FN = NP // FB
    assert NG * GW == NW
    assert NP == FB * FN + 1
    assert NW * WN == N and 2 * NP == NW and ER * WN == E and N <= NOWHERE

    RP = N // P
    LR = 4
    NCH = RP // LR
    REST = N - RP * P
    assert NCH * LR == RP

    with ExitStack() as ctx:
        def sb(name, shape, dt=F32):
            return ctx.enter_context(nc.sbuf_tensor(name, shape, dt))

        def sem(name):
            return ctx.enter_context(nc.semaphore(name))

        def dram(name, shape, dt):
            return nc.dram_tensor(name, shape, dt).ap()

        table = dram("table", [N, 2 * C], F16)
        srcp = dram("srcp", [EP], I32)
        dstp = dram("dstp", [EP], I32)
        sums = dram("sums", [N, C], F32)
        res = dram("res", [N, C], F32)
        swt_d = dram("swt_d", [NP, P, 2 * KT * WN], F32)

        wih_h = sb("wih_h", [P, KT, MT, P], F32R)
        wih_l = sb("wih_l", [P, KT, MT, P], F32R)
        w1_h = sb("w1_h", [P, 2 * CT, HID], F32R)
        w1_l = sb("w1_l", [P, 2 * CT, HID], F32R)
        wfc_h = sb("wfc_h", [P, KT, C], F32R)
        wfc_l = sb("wfc_l", [P, KT, C], F32R)
        wxs_h = sb("wxs_h", [P, CT, HG], F32R)
        wxs_l = sb("wxs_l", [P, CT, HG], F32R)
        ring = sb("ring", [P, 2, CH, 2 * C], F16)
        oneh = sb("oneh", [P, 2, CH, P], F16)
        hf = sb("hf", [P, KT, 2 * P])
        h_h = sb("h_h", [P, KT, 2 * P], F32R)
        h_l = sb("h_l", [P, KT, 2 * P], F32R)
        hl_h = sb("hl_h", [P, KT, 2 * P], F32R)
        hl_l = sb("hl_l", [P, KT, 2 * P], F32R)
        at_h = sb("at_h", [P, CT, 2 * P], F32R)
        at_l = sb("at_l", [P, CT, 2 * P], F32R)
        xt_h = sb("xt_h", [P, CT, 2 * P], F32R)
        xt_l = sb("xt_l", [P, CT, 2 * P], F32R)
        agg = sb("agg", [P, 2, C])
        xn16 = sb("xn16", [P, 2, 2 * C], F16)
        xin = sb("xin", [P, 2, C])
        x2 = sb("x2", [P, 2, C])
        x2_h = sb("x2_h", [P, 2, C], F32R)
        x2_l = sb("x2_l", [P, 2, C], F32R)
        x2t_h = sb("x2t_h", [P, CT, 2 * P], F32R)
        x2t_l = sb("x2t_l", [P, CT, 2 * P], F32R)
        gate = sb("gate", [P, 3, KT, 2 * P])
        sw = sb("sw", [P, 2, HG])
        sw_h = sb("sw_h", [P, 2, HG], F32R)
        sw_l = sb("sw_l", [P, 2, HG], F32R)
        norm = sb("norm", [P, HG])
        swt = sb("swt", [P, 2, KT, WN])
        biasx = sb("biasx", [P, HG])
        ident = sb("ident", [P, P])
        ident16 = sb("ident16", [P, P], F16)
        iota = sb("iota", [P, P], F16)
        wbase = sb("wbase", [P, NW + 2])
        rel = sb("rel", [P, 2, CH])
        sidx = sb("sidx", [P, 2, CH], I32)
        didx = sb("didx", [P, 2, CH], I32)
        ones = sb("ones", [P, 1])
        bfc = sb("bfc", [P, C])
        bout = sb("bout", [P, C])
        brel = sb("brel", [P, KT])
        bgate = sb("bgate", [P, KT, 3])
        braw = sb("braw", [P, 2, 3, KT])
        temp8 = sb("temp8", [P, H])
        rtemp = sb("rtemp", [P, H])
        extra = sb("extra", [P, 2, C])
        stats = sb("stats", [P, 2, LR, 6])
        mv = sb("mv", [P, 2, LR, 2])
        sd = sb("sd", [P, 2, LR])
        rstd = sb("rstd", [P, 2, LR])
        nmr = sb("nmr", [P, 2, LR])
        eps = sb("eps", [P, 1])
        mx8 = sb("mx8", [P, 2 * H])
        sm8 = sb("sm8", [P, 2 * H])
        rs8 = sb("rs8", [P, 2 * H])
        base_i = sb("base_i", [1, NW + 2], I32)
        flag_i = sb("flag_i", [1, 1], I32)
        col = sb("col", [P, 8])
        coli = sb("coli", [P, 1], I32)

        scratch = ring[:, :, :, :].rearrange("p a b c -> p (a b c)").bitcast(F32)
        words = LR * C
        lx = [scratch[:, k * words:(k + 1) * words].rearrange("p (r c) -> p r c", c=C) for k in range(3)]
        ln = [scratch[:, (3 + k) * words:(4 + k) * words].rearrange("p (r c) -> p r c", c=C) for k in range(2)]
        lt = [scratch[:, (5 + k) * words:(6 + k) * words].bitcast(F16).rearrange("p (r c) -> p r c", c=2 * C)
              for k in range(2)]
        edge_i = scratch[:, 7 * words:7 * words + ER + 1].bitcast(I32)
        lt.append(scratch[:, 8600:8600 + C].bitcast(F16).rearrange("p (r c) -> p r c", c=2 * C))
        row = scratch[0:1, 8100:8100 + 5 * (NW + 2)].rearrange("p (k n) -> p k n", k=5)
        pick = scratch[:, 8400:8400 + NW + 2]
        hot_words = oneh[:, :, :, :].rearrange("p a b c -> p (a b c)").bitcast(F32)
        edge_f = hot_words[:, 0:ER + 1]
        edge_le = hot_words[:, 1000:1000 + ER]
        raw = gate[:, :, :, :].rearrange("p a b c -> p (a b c)")
        wx_raw = sw[:, :, :]
        wxt = hf[:, :, :]
        wsl = swt[:, :, :, :].rearrange("p a b c -> p (a b c)")[:, 0:G]
        bsl = swt[:, :, :, :].rearrange("p a b c -> p (a b c)")[:, 64:64 + G]
        bxc = swt[:, :, :, :].rearrange("p a b c -> p (a b c)")[:, 128:128 + KT]
        bxb = swt[:, :, :, :].rearrange("p a b c -> p (a b c)")[:, 256:256 + KT * P].rearrange(
            "p (k n) -> p k n", n=P)

        at = 0

        def carve(parts, n):
            nonlocal at
            at += n
            assert at <= 9216
            return scratch[0:parts, at - n:at]

        wfx = carve(P, CT * HG).rearrange("p (k n) -> p k n", k=CT)
        tks = carve(P, CT * HG).rearrange("p (k n) -> p k n", k=CT)
        wout = carve(D, H * C).rearrange("p (h n) -> p h n", h=H)
        wqkv = carve(D, 3 * D).rearrange("p (k n) -> p k n", k=3)
        bfx, tokens, tokt, qt, kt, vv, att, attt, tmp = (carve(G, HG) for _ in range(9))
        ost = tokens
        flat_swt = swt[:, :, :, :].rearrange("p a b c -> p (a b c)")
        fsw = [raw[:, k * 1024:k * 1024 + 2 * KT * WN] for k in range(3)] + [flat_swt]
        fres = [hf[:, 2 * k:2 * k + 2, :].rearrange("p a b -> p (a b)").rearrange("p (e c) -> p e c", e=2)
                for k in range(2)] + [x2[:, :, :], xin[:, :, :]]
        fo = [sw[:, k, :].rearrange("p (e c) -> p e c", e=2) for k in range(2)] + [agg[:, :, :], extra[:, :, :]]
        wih_hf, wih_lf = (w[:, :, :, :].rearrange("p a b c -> p (a b c)") for w in (wih_h, wih_l))
        fsw_h, fsw_l = ([w[:, k * 1024:k * 1024 + 2 * KT * WN] for k in range(FB)] for w in (wih_hf, wih_lf))
        v_h, v_l = (w[:, FB * 1024:(FB + 1) * 1024].rearrange("p (j c) -> p j c", c=C) for w in (wih_hf, wih_lf))

        ps = ctx.enter_context(nc.psum_tensor("ps", [P, 8, 512], F32))
        SUM_A, SUM_B, XA, XX, HA, HB, TOK = 0, 1, 2, 3, 4, 5, 6
        gen_bank = (SUM_A, SUM_B, XA, XX, HA)
        f_bank = (TOK, TOK + 1, HA, HB)
        xx16 = ps[:, XX, :].bitcast(F16).rearrange("p (h q n) -> p h q n", h=2, q=2)

        ld_edges, ld_pads, ld_tab = sem("ld_edges"), sem("ld_pads"), sem("ld_tab")
        ld_small, ld_w1, ld_wih, ld_wx, ld_wfc = (sem(n) for n in ("ld_small", "ld_w1", "ld_wih", "ld_wx", "ld_wfc"))
        ld_rows = sem("ld_rows")
        ln_in = [sem(f"ln_in{k}") for k in range(3)]
        ln_out = [sem(f"ln_out{k}") for k in range(2)]
        consts, dve_step, pe_step, pool_step = (
            sem(n) for n in ("consts", "dve_step", "pe_step", "pool_step"))
        pads_set, plan_m, plan_pw, plan_row, plan_cnt, plan_t, plan_done = (
            sem(n) for n in ("pads_set", "plan_m", "plan_pw", "plan_row", "plan_cnt", "plan_t", "plan_done"))
        ln_var, ln_sd, ln_rstd, ln_x, ln_hi = (
            sem(n) for n in ("ln_var", "ln_sd", "ln_rstd", "ln_x", "ln_hi"))
        ln_lo = [sem(f"ln_lo{k}") for k in range(2)]
        w1_free, wprep_t, wprep_h, wprep_l, wxt_t, wxt_c, wxs_m, wxs_c, w_ready = (
            sem(n) for n in ("w1_free", "wprep_t", "wprep_h", "wprep_l", "wxt_t", "wxt_c", "wxs_m", "wxs_c", "w_ready"))
        gather_go = sem("gather_go")
        gen_idx, gen_rel, gen_hot, gen_mm, gen_zero, gen_high, gen_sum, gen_st = (
            sem(n) for n in ("gen_idx", "gen_rel", "gen_hot", "gen_mm", "gen_zero", "gen_high", "gen_sum", "gen_st"))
        gen_rows = [sem(f"gen_rows{k}") for k in range(3)]
        idx_in = [sem(f"idx_in{e}") for e in range(2)]
        rel_done = [sem(f"rel_done{e}") for e in range(2)]
        hot_done = [sem(f"hot_done{e}") for e in range(2)]
        rows_in = [[sem(f"rows_in{e}{k}") for k in range(2)] for e in range(2)]
        half_used = [sem(f"half_used{e}") for e in range(2)]
        sum_done = [sem(f"sum_done{e}") for e in range(2)]
        agg_done = [sem(f"agg_done{e}") for e in range(2)]
        gen_in = sem("gen_in")
        xn_in, x_in = sem("xn_in"), sem("x_in")
        xt_done, xsplit_a, xsplit_v = sem("xt_done"), sem("xsplit_a"), sem("xsplit_v")
        h_mm, h_act, h_hi, h_lo = sem("h_mm"), sem("h_act"), sem("h_hi"), sem("h_lo")
        gate_mm, gate_act, cell_v, cell_t, cell_out, hl_hi, hl_lo = (
            sem(n) for n in ("gate_mm", "gate_act", "cell_v", "cell_t", "cell_out", "hl_hi", "hl_lo"))
        y_mm, x2_step, var_done, sd_done, rstd_done, res_done, res_st = (
            sem(n) for n in ("y_mm", "x2_step", "var_done", "sd_done", "rstd_done", "res_done", "res_st"))
        x2_norm, x2_hi, x2_lo, x2t_mm, x2t_hi, x2t_lo = (
            sem(n) for n in ("x2_norm", "x2_hi", "x2_lo", "x2t_mm", "x2t_hi", "x2t_lo"))
        lg_mm, lg_sub, lg_exp, sm_step, sw_done, norm_add, sw_hi, sw_lo = (
            sem(n) for n in ("lg_mm", "lg_sub", "lg_exp", "sm_step", "sw_done", "norm_add", "sw_hi", "sw_lo"))
        swt_mm, swt_done, swt_st, tok_mm = sem("swt_mm"), sem("swt_done"), sem("swt_st"), sem("tok_mm")
        ld_att, att_pe, att_v, att_a = sem("ld_att"), sem("att_pe"), sem("att_v"), sem("att_a")
        f_in = [sem(f"f_in{k}") for k in range(FB)]
        f_res = [sem(f"f_res{k}") for k in range(FB)]
        f_st = [sem(f"f_st{k}") for k in range(FB)]
        f_hi = [sem(f"f_hi{k}") for k in range(FB)]
        f_lo = [sem(f"f_lo{k}") for k in range(FB)]
        f_mm = [sem(f"f_mm{k}") for k in range(FB)]
        f_out = [sem(f"f_out{k}") for k in range(FB)]

        gen_add = sem("gen_add")
        low_out = [sem(f"low_out{e}") for e in range(2)]
        V_TKS, V_TOKENS, V_TOKT, V_QK, ATT_SUB, V_ATT, V_V, V_ATTT, V_OST, V_VLO = 1, 7, 8, 10, 12, 15, 16, 17, 18, 20
        PE_V = 9

        block = ctx.enter_context(nc.Block())

        def pair_rows(t, p, width):
            return t[ds(p * (2 * WN), 2 * WN), :].rearrange("(e n) c -> n e c", n=WN)

        PARTS = ((0, 112), (112, WN))

        def turns(turn):
            turn(0, True, False, False, True)
            turn(1, True, True, False, True)
            turn(2, True, True, True, True)
            return (3, NP - 1)

        def last_turns(turn):
            turn(NP - 1, True, True, True, False)
            turn(NP, False, True, True, False)
            turn(NP + 1, False, False, True, False)


        def three(eng, dst, wh, wl, xh, xl, first, last):
            eng.matmul(dst, wh, xh, start=first, stop=False)
            eng.matmul(dst, wh, xl, start=False, stop=False)
            return eng.matmul(dst, wl, xh, start=False, stop=last)


        @block.sync
        def _(sp):
            sp.dma_start(srcp[0:E].rearrange("(a b) -> a b", b=ER), a["src"].rearrange("(a b) -> a b", b=ER)).then_inc(ld_edges, 16)
            sp.dma_start(dstp[0:E].rearrange("(a b) -> a b", b=ER), a["dst"].rearrange("(a b) -> a b", b=ER)).then_inc(ld_edges, 16)

            def load_chunk(k):
                if k >= 3:
                    sp.wait_ge(ln_x, LR * (k - 2))
                if k < NCH:
                    src = a["x"][0:RP * P, :].rearrange("(p r) c -> p r c", p=P)[:, k * LR:(k + 1) * LR, :]
                    sp.dma_start(lx[k % 3], src).then_inc(ln_in[k % 3], 16)
                else:
                    sp.dma_start(lx[k % 3][0:REST, 0, :], a["x"][RP * P:N, :]).then_inc(ln_in[k % 3], 16)

            def store_chunk(k):
                sp.wait_ge(ln_hi, k + 1)
                sp.wait_ge(ln_lo[k % 2], k // 2 + 1)
                if k < NCH:
                    dst = table[0:RP * P, :].rearrange("(p r) c -> p r c", p=P)[:, k * LR:(k + 1) * LR, :]
                    sp.dma_start(dst, lt[k % 2]).then_inc(ln_out[k % 2], 16)
                else:
                    sp.dma_start(table[RP * P:N, :], lt[2][0:REST, 0, :]).then_inc(ln_out[k % 2], 16)

            load_chunk(0)
            load_chunk(1)
            load_chunk(2)
            with nc.allow_non_contiguous_dma(reason="bias vectors go down the partitions once"):
                sp.dma_start(brel[:, :], a["b_rel"].rearrange("(k p) -> p k", p=P)).then_inc(ld_small, 16)
                for j, g in enumerate(GATES):
                    for q, b in enumerate(("b_ih", "b_hh")):
                        v = a[b][g * HID:(g + 1) * HID].rearrange("(k p) -> p k", p=P)
                        sp.dma_start(braw[:, q, j, :], v).then_inc(ld_small, 16)
                sp.dma_start(bxc, a["b_x"].rearrange("(k p) -> p k", p=P)).then_inc(ld_small, 16)
            sp.dma_start(bfc[:, :], a["b_fc"].partition_broadcast(P)).then_inc(ld_small, 16)
            sp.dma_start(bout[:, :], a["b_out"].partition_broadcast(P)).then_inc(ld_small, 16)
            sp.dma_start(bsl, a["b_slice"].partition_broadcast(P)).then_inc(ld_small, 16)
            sp.dma_start(temp8[:, :], a["temperature"].rearrange("a h b c -> (a h b c)").partition_broadcast(P)).then_inc(ld_small, 16)
            for k in range(2):
                sp.dma_start(wsl[k * D:(k + 1) * D, :], a["W_slice"]).then_inc(ld_small, 16)
            sp.dma_start(wx_raw, a["W_x"].rearrange("(k p) n -> p k n", p=P)).then_inc(ld_wx, 16)
            sp.wait_ge(pads_set, 2)
            for idx, t in ((sidx, srcp), (didx, dstp)):
                sp.dma_start(t[E:EP].rearrange("(p b) -> p b", p=P), idx[:, 0, :]).then_inc(ld_pads, 16)
            sp.wait_ge(ld_edges, 32)
            sp.wait_ge(ld_pads, 32)
            rows = dstp[0:E].rearrange("(p b) -> p b", b=ER)
            nxt = dstp[ER:E + ER].rearrange("(p b) -> p b", b=ER)
            sp.dma_start(edge_i[0:WN, 0:ER], rows).then_inc(ld_tab, 16)
            with nc.allow_non_contiguous_dma(reason="one element a row"):
                sp.dma_start(edge_i[0:WN, ER:ER + 1], nxt[:, 0:1]).then_inc(ld_tab, 16)
            r4 = raw[:, 0:4 * HID].rearrange("p (k n) -> p k n", n=HID)
            for k in range(NCH + 1):
                if k + 3 <= NCH:
                    load_chunk(k + 3)
                if k >= 1:
                    store_chunk(k - 1)
                if k == NCH - 2:
                    sp.dma_start(r4[:, 0:CT, :], a["W_rel"].rearrange("(k p) n -> p k n", p=P)).then_inc(ld_w1, 16)
                    sp.dma_start(r4[:, CT:2 * CT, :], a["W_root"].rearrange("(k p) n -> p k n", p=P)).then_inc(ld_w1, 16)
            store_chunk(NCH)

            sp.wait_ge(plan_done, 2)
            general = sp.value_load(flag_i[0:1, 0:1], min_val=0, max_val=1)

            def load_edges(base, e, done):
                for idx, t in ((sidx, srcp), (didx, dstp)):
                    sp.dma_start(idx[:, e, :], t[ds(base, CAP)].rearrange("(p j) -> p j", p=P)).then_inc(done, 16)

            with sp.If(general):
                sp.sem_inc(gen_st, 16)
                with sp.Fori(0, NG) as g:
                    with sp.Fori(0, ROUNDS) as r:
                        sp.wait_ge(gen_mm, (g * ROUNDS + r) * GW + 2)
                        load_edges(r * CAP, 0, gen_idx)
                    for i in range(GW):
                        sp.wait_ge(gen_sum, g * GW + i + 2)
                        sp.dma_start(sums[ds((g * GW + i) * WN, WN), :], agg[0:WN, 0, :]).then_inc(gen_st, 16)
                sp.wait_ge(gen_st, 16 * NW + 16)

            def edges(p, e):
                w = 2 * p + e
                if not (isinstance(p, int) and p == 0):
                    sp.wait_ge(rows_in[e][0], 16 * HALF * p)
                    sp.wait_ge(rows_in[e][1], 16 * HALF * p)
                    sp.wait_ge(rel_done[e], p)
                base = sp.value_load(base_i[0:1, ds(w, 1)], min_val=0, max_val=E)
                load_edges(base, e, idx_in[e])

            def turn(t, gather, gnn, ffn, ahead):
                if gather:
                    if not (isinstance(t, int) and t == 0):
                        sp.wait_ge(xt_done, t)
                    for u, v in PARTS:
                        sp.dma_start(xn16[u:v, :, :], pair_rows(table, t, 2 * C)[u:v]).then_inc(xn_in, 16)
                    with sp.If(general):
                        sp.wait_ge(gen_add, 2 * t)
                        for u, v in PARTS:
                            sp.dma_start(extra[u:v], pair_rows(sums, t, C)[u:v]).then_inc(gen_in, 16)
                if ahead:
                    edges(t + 1, 0)
                if ffn:
                    p = t - 2
                    sp.wait_ge(res_done, p + 1)
                    for u, v in PARTS:
                        sp.dma_start(pair_rows(res, p, C)[u:v], xin[u:v, :, :]).then_inc(res_st, 16)
                if gnn:
                    p = t - 1
                    if not (isinstance(p, int) and p == 0):
                        sp.wait_ge(res_st, 32 * p)
                    for u, v in PARTS:
                        sp.dma_start(xin[u:v, :, :], pair_rows(a["x"], p, C)[u:v]).then_inc(x_in, 16)
                if ahead:
                    edges(t + 1, 1)

            edges(0, 0)
            edges(0, 1)
            sp.wait_ge(w1_free, 2)
            for q in range(2):
                if q:
                    sp.wait_ge(wprep_t, MT // 2)
                for n in range(q * MT // 2, (q + 1) * MT // 2):
                    f, g = n // 3, GATES[n % 3]
                    r = g * HID + f * P
                    s = n % (MT // 2)
                    sp.dma_start(raw[:, s * HID:(s + 1) * HID], a["W_ih"][r:r + P, :]).then_inc(ld_wih, 16)
            sp.wait_ge(wprep_t, MT)
            sp.dma_start(raw[:, 0:KT * C].rearrange("p (k n) -> p k n", n=C),
                         a["W_fc"].rearrange("(k p) n -> p k n", p=P)).then_inc(ld_wfc, 16)
            lo, hi = turns(turn)
            with sp.Fori(lo, hi) as t:
                turn(t, True, True, True, True)
            last_turns(turn)
            sp.wait_ge(res_st, 32 * NP)
            sp.wait_ge(swt_st, 16 * NP)

            sp.wait_ge(sum_done[1], NP)
            sp.dma_start(wfx, a["W_fx"].rearrange("(k p) n -> p k n", p=P)).then_inc(ld_att, 16)
            sp.dma_start(wout, a["W_out"].rearrange("(h p) n -> p h n", p=D)).then_inc(ld_att, 16)
            for k, n in enumerate(("W_q", "W_k", "W_v")):
                sp.dma_start(wqkv[:, k, :], a[n]).then_inc(ld_att, 16)
            sp.dma_start(bfx, a["b_fx"].partition_broadcast(G)).then_inc(ld_att, 16)

            def f_load(n, k):
                p = FB * n + k
                if not (isinstance(n, int) and n == 0):
                    sp.wait_ge(f_hi[k], n)
                    sp.wait_ge(f_lo[k], n)
                sp.dma_start(fsw[k], swt_d[ds(p, 1)].rearrange("a p n -> p (a n)")).then_inc(f_in[k], 16)
                if not (isinstance(n, int) and n == 0):
                    sp.wait_ge(f_out[k], n + 1)
                for u, v in PARTS:
                    sp.dma_start(fres[k][u:v], pair_rows(res, p, C)[u:v]).then_inc(f_res[k], 16)

            sp.wait_ge(cell_out, KT * NP)
            sp.wait_ge(hl_lo, 2 * NP)
            sp.wait_ge(x2t_mm, NP)
            sp.wait_ge(x2_lo, NP)
            for k in range(FB):
                f_load(0, k)
            with sp.Fori(1, FN) as n:
                for k in range(FB):
                    f_load(n, k)
            f_load(FN, 0)
            for k in range(FB):
                sp.wait_ge(f_st[k], 32 * (FN + (k == 0)))

        def after(eng, s, n):
            if not (isinstance(n, int) and n <= 0):
                eng.wait_ge(s, n)

        def valid(x):
            return x.rearrange("p k (e n) -> p (k e) n", n=P)[:, :, 0:WN]

        def bank_valid(b):
            return ps[:, b, :].rearrange("p (q n) -> p q n", n=P)[:, :, 0:WN]

        NCONST = 8

        def ln_low(eng, k):
            n, rows = (P, LR) if k < NCH else (REST, 1)
            q = k % 2
            eng.wait_ge(ln_x, min(LR * (k + 1), LR * NCH + 1))
            eng.wait_ge(ln_hi, k + 1)
            to = lt[q if k < NCH else 2]
            eng.tensor_tensor(to[0:n, 0:rows, C:2 * C], ln[q][0:n, 0:rows, :], to[0:n, 0:rows, 0:C],
                              ALU.subtract).then_inc(ln_lo[q], 1)

        @block.gpsimd
        def _(pool):
            pool.memset(ident[:, :], 0.0).then_inc(pool_step, 1)
            pool.iota(iota[:, :], [[1, P]], base=0, channel_multiplier=0,
                      allow_small_or_imprecise_dtypes=True).then_inc(consts, 1)
            pool.iota(wbase[:, :], [[WN, NW + 2]], base=0, channel_multiplier=0,
                      allow_small_or_imprecise_dtypes=True).then_inc(consts, 1)
            pool.iota(col[:, 7:8], [[0, 1]], base=0, channel_multiplier=WN,
                      allow_small_or_imprecise_dtypes=True).then_inc(consts, 1)
            pool.memset(ones[:, :], 1.0).then_inc(consts, 1)
            pool.memset(eps[:, :], EPS).then_inc(consts, 1)
            pool.iota(sidx[:, 0, :], [[0, CH]], base=0, channel_multiplier=0).then_inc(pads_set, 1)
            pool.iota(didx[:, 0, :], [[0, CH]], base=NOWHERE, channel_multiplier=0).then_inc(pads_set, 1)
            pool.wait_ge(pool_step, 1)
            pool.affine_select(out=ident[:, :], in_=ident[:, :], compare_op=ALU.not_equal, fill=1.0,
                               base=0, pattern=[[-1, P]], channel_multiplier=1).then_inc(consts, 1)
            for x in (at_h, at_l, xt_h, xt_l):
                pool.memset(x[:, :, :].bitcast(F32), 0.0).then_inc(w_ready, 1)
            pool.memset(norm[:, :], 0.0).then_inc(consts, 1)
            pool.memset(pick[:, :], 0.0).then_inc(consts, 1)

            ln_low(pool, 1)
            ln_low(pool, 3)
            pool.wait_ge(plan_row, 1)
            pool.indirect_dma_start(edge_i[0:NW + 1, 0:ER], None, dstp[0:E].rearrange("(p b) -> p b", b=ER),
                                    bass.IndirectOffsetOnAxis(ap=coli[0:NW + 1, 0:1], axis=0)).then_inc(ld_rows, 16)
            for k in range(5, NCH - 1, 2):
                ln_low(pool, k)
            pool.wait_ge(ln_out[0], 16 * ((NCH + 2) // 2))
            pool.wait_ge(ln_out[1], 16 * ((NCH + 1) // 2))
            pool.wait_ge(plan_done, 2)
            general = pool.value_load(flag_i[0:1, 0:1], min_val=0, max_val=1)

            def gather(e, j, done):
                pool.indirect_dma_start(ring[:, e, j, :], None, table,
                                        bass.IndirectOffsetOnAxis(ap=sidx[:, e, j:j + 1], axis=0)).then_inc(done, 16)

            with pool.If(general):
                with pool.Fori(0, NG) as g:
                    with pool.Fori(0, ROUNDS) as r:
                        n = g * ROUNDS + r
                        pool.wait_ge(gen_idx, n * 32 + 32)
                        pool.wait_ge(gen_mm, n * GW + 2)
                        pool.sem_inc(gather_go, 1)
                        for j in range(CH):
                            gather(0, j, gen_rows[j % 3])
                pool.wait_ge(gen_mm, NG * ROUNDS * GW + 2)

            def gathers(p):
                for e in range(2):
                    for k, used in enumerate((half_used[e], sum_done[e])):
                        if k == 0:
                            pool.wait_ge(idx_in[e], 32 * p + 32)
                        after(pool, used, p)
                        pool.sem_inc(gather_go, 1)
                        for j in range(k * HALF, (k + 1) * HALF):
                            gather(e, j, rows_in[e][k])

            gathers(0)
            with pool.Fori(1, NP) as p:
                gathers(p)

            def f_store(n, k):
                p = FB * n + k
                pool.wait_ge(f_out[k], n + 2)
                for u, v in PARTS:
                    pool.dma_start(pair_rows(out, p, C)[u:v], fo[k][u:v]).then_inc(f_st[k], 16)

            with pool.Fori(0, FN) as n:
                for k in range(FB):
                    f_store(n, k)
            f_store(FN, 0)
            for k in range(FB):
                pool.wait_ge(f_st[k], 32 * (FN + (k == 0)))

        @block.scalar
        def _(act):
            act.wait_ge(consts, NCONST)
            def ln_dev(k):
                n, rows = (P, LR) if k < NCH else (REST, 1)
                act.wait_ge(ln_var, k + 1)
                act.activation(sd[0:n, k % 2, 0:rows], mv[0:n, k % 2, 0:rows, 1], ACT.Sqrt,
                               bias=eps[0:n, :]).then_inc(ln_sd, 1)

            ln_dev(0)
            for k in range(NCH + 1):
                n, rows = (P, LR) if k < NCH else (REST, 1)
                q = k % 2
                act.wait_ge(ln_rstd, k + 1)
                if k >= 2:
                    act.wait_ge(ln_hi, k - 1)
                    act.wait_ge(ln_lo[q], k // 2)
                for r in range(rows):
                    act.activation(ln[q][0:n, r, :], lx[k % 3][0:n, r, :], ACT.Identity,
                                   bias=nmr[0:n, q, r:r + 1], scale=rstd[0:n, q, r:r + 1]).then_inc(ln_x, 1)
                if k < NCH:
                    ln_dev(k + 1)
                act.wait_ge(ln_x, min(LR * (k + 1), LR * NCH + 1))
                if 2 <= k < NCH:
                    act.wait_ge(ln_out[q], 16 * (k // 2))
                act.activation(lt[q if k < NCH else 2][0:n, 0:rows, 0:C], ln[q][0:n, 0:rows, :], ACT.Copy).then_inc(ln_hi, 1)
            act.wait_ge(ld_w1, 32)
            act.activation(w1_h[:, :, :], raw[:, 0:4 * HID].rearrange("p (k n) -> p k n", n=HID), ACT.Copy).then_inc(w1_free, 1)
            act.wait_ge(wxs_c, 2)
            act.activation(wxs_h[:, :, :], sw[:, :, :], ACT.Copy).then_inc(wprep_h, 1)
            for n in range(MT):
                act.wait_ge(wprep_t, n + 1)
                act.activation(wih_h[:, :, n, :], ps[:, XA + n % 2, :].rearrange("p (k m) -> p k m", m=P),
                               ACT.Copy).then_inc(wprep_h, 1)
            act.wait_ge(ld_wfc, 16)
            act.activation(wfc_h[:, :, :], raw[:, 0:KT * C].rearrange("p (k n) -> p k n", n=C), ACT.Copy,
                           scale=0.5).then_inc(wprep_h, 1)

            def split_x(p):
                act.wait_ge(xt_done, p + 1)
                act.activation(valid(at_h[:, :, :]), bank_valid(XA), ACT.Copy).then_inc(xsplit_a, 1)
                for q, x in enumerate((xt_h, xt_l)):
                    for hh in range(CT):
                        act.activation(x[:, hh, :].rearrange("p (e n) -> p e n", n=P)[:, :, 0:WN],
                                       xx16[:, hh, q, :].rearrange("p (e n) -> p e n", n=P)[:, :, 0:WN],
                                       ACT.Copy).then_inc(xsplit_a, 1)

            def dev_x2(p):
                act.wait_ge(var_done, 2 * p + 2)
                act.activation(sd[0:WN, 0, 0:2], mv[0:WN, 0, 0:2, 1], ACT.Sqrt, bias=eps[0:WN, :]).then_inc(sd_done, 1)

            def norm_x2(p):
                act.wait_ge(rstd_done, 2 * p + 2)
                act.wait_ge(res_done, p + 1)
                for e in range(2):
                    act.activation(x2[0:WN, e, :], x2[0:WN, e, :], ACT.Identity,
                                   bias=nmr[0:WN, 0, e:e + 1], scale=rstd[0:WN, 0, e:e + 1]).then_inc(x2_norm, 1)
                act.wait_ge(x2_norm, 2 * p + 2)
                after(act, tok_mm, p)
                act.activation(x2_h[0:WN, :, :], x2[0:WN, :, :], ACT.Copy).then_inc(x2_hi, 1)

            def relu_h(p, q):
                if q == 0:
                    after(act, hl_lo, 2 * p)
                act.wait_ge(h_mm, 2 * p + q + 1)
                for m in (2 * q, 2 * q + 1):
                    act.activation(hf[:, m, :], ps[:, HA + q, (m % 2) * 256:(m % 2) * 256 + 256], ACT.Relu,
                                   bias=brel[:, m:m + 1]).then_inc(h_act, 1)
                act.wait_ge(h_act, KT * p + 2 * q + 2)
                act.activation(h_h[:, 2 * q:2 * q + 2, :], hf[:, 2 * q:2 * q + 2, :], ACT.Copy).then_inc(h_hi, 1)

            def split_x2t(p):
                act.wait_ge(x2t_mm, p + 1)
                act.activation(valid(x2t_h[:, :, :]), bank_valid(XX), ACT.Copy).then_inc(x2t_hi, 1)

            def gates(p, first, end):
                for n in range(first, end):
                    f, g = n // 3, n % 3
                    act.wait_ge(gate_mm, MT // 2 * p + n // 2 + 1)
                    if n == 0:
                        after(act, cell_out, KT * p)
                    s = n % 4
                    act.activation(gate[:, g, f, :], ps[:, HA + s // 2, (s % 2) * 256:(s % 2) * 256 + 256], ACT.Tanh,
                                   bias=bgate[:, f, g:g + 1], scale=1.0 if g == 1 else 0.5).then_inc(gate_act, 1)

            def tanh_c(p, f):
                act.wait_ge(cell_v, KT * p + f + 1)
                act.activation(gate[:, 1, f, :], gate[:, 0, f, :], ACT.Tanh, scale=0.5).then_inc(cell_t, 1)

            def copy_swt(p, e):
                act.wait_ge(swt_mm, 2 * p + e + 1)
                act.activation(swt[:, e, :, :], bank_valid(XA + e), ACT.Copy).then_inc(swt_done, 1)

            def high_hl(p, q):
                if q == 0:
                    after(act, y_mm, p)
                act.wait_ge(cell_out, KT * p + 2 * q + 2)
                act.activation(hl_h[:, 2 * q:2 * q + 2, :], hf[:, 2 * q:2 * q + 2, :], ACT.Copy).then_inc(hl_hi, 1)

            def turn(t, gather, gnn, ffn, ahead):
                if gnn:
                    split_x(t - 1)
                    relu_h(t - 1, 0)
                if ffn:
                    dev_x2(t - 2)
                if gnn:
                    relu_h(t - 1, 1)
                if ffn:
                    norm_x2(t - 2)
                    split_x2t(t - 2)
                if gnn:
                    gates(t - 1, 0, 4)
                    tanh_c(t - 1, 0)
                if ffn:
                    act.wait_ge(lg_sub, t - 1)
                    act.activation(sw[0:WN, :, :], sw[0:WN, :, :], ACT.Exp).then_inc(lg_exp, 1)
                if gnn:
                    gates(t - 1, 4, 8)
                    tanh_c(t - 1, 1)
                    gates(t - 1, 8, 10)
                if ffn:
                    p = t - 2
                    act.wait_ge(sw_done, p + 1)
                    after(act, tok_mm, p)
                    act.activation(sw_h[0:WN, :, :], sw[0:WN, :, :], ACT.Copy).then_inc(sw_hi, 1)
                if gnn:
                    tanh_c(t - 1, 2)
                    gates(t - 1, 10, 12)
                    high_hl(t - 1, 0)
                    tanh_c(t - 1, 3)
                if ffn:
                    after(act, swt_st, 16 * (t - 2))
                    copy_swt(t - 2, 0)
                if gnn:
                    high_hl(t - 1, 1)
                if ffn:
                    p = t - 2
                    copy_swt(p, 1)
                    act.wait_ge(swt_done, 2 * p + 2)
                    act.dma_start(swt_d[ds(p, 1)].rearrange("a p n -> p (a n)"),
                                  swt[:, :, :, :].rearrange("p e j n -> p (e j n)")).then_inc(swt_st, 16)

            lo, hi = turns(turn)
            with act.Fori(lo, hi) as t:
                turn(t, True, True, True, True)
            last_turns(turn)

            def f_high(n, k):
                act.wait_ge(f_in[k], 16 * n + 16)
                act.wait_ge(f_mm[k], n + 1)
                act.activation(fsw_h[k], fsw[k], ACT.Copy).then_inc(f_hi[k], 1)

            act.wait_ge(tok_mm, NP)
            for k in range(FB):
                f_high(0, k)
            act.wait_ge(att_v, ATT_SUB)
            act.activation(att[:, :], att[:, :], ACT.Exp, scale=SCALE).then_inc(att_a, 1)
            act.wait_ge(att_pe, PE_V)
            for b in range(2):
                act.activation(v_h[:, 2 * b:2 * b + 2, :], ps[:, 3 + b, :].rearrange("p (j c) -> p j c", c=C),
                               ACT.Copy).then_inc(att_a, 1)

            with act.Fori(1, FN) as n:
                for k in range(FB):
                    f_high(n, k)
            f_high(FN, 0)

        @block.tensor
        def _(pe):
            pe.wait_ge(consts, NCONST)
            pe.wait_ge(w_ready, 4)
            zeros = at_h[:, :, :].rearrange("p k n -> p (k n)")
            for b in (TOK, TOK + 1):
                pe.matmul(ps[:, b, :], zeros[:, 0:P], zeros, start=True, stop=False)
            pe.wait_ge(plan_m, 2)
            pe.matmul(ps[0:NW + 1, 0, 0:1], pick[0:WN, 0:NW + 1], ones[0:WN, 0:1], start=True, stop=True)
            pe.matmul(ps[0:1, 1, 0:1], col[0:WN, 0:1], ones[0:WN, 0:1], start=True, stop=True).then_inc(plan_pw, 1)
            pe.wait_ge(ld_wx, 16)
            for ct in range(CT):
                for j in range(KT):
                    last = pe.transpose(ps[:, XA + ct, j * P:(j + 1) * P], wx_raw[:, ct, j * P:(j + 1) * P], ident[:, :])
            last.then_inc(wxt_t, 1)
            pe.wait_ge(wxt_c, 2)
            wx4 = wxt.rearrange("p a b -> p (a b)").rearrange("p (c j n) -> p c j n", c=CT, j=KT)
            for h in (*range(0, H, 2), *range(1, H, 2)):
                u = (h % 2) * D
                if h == 1:
                    pe.wait_ge(pe_step, 1)
                for ct in range(CT):
                    pe.matmul(ps[:, HA + ct, h * G:(h + 1) * G], wx4[u:u + D, ct, h // 2, :], wsl[u:u + D, :],
                              start=True, stop=True)
                last = pe.matmul(ps[:, XA, h * G:(h + 1) * G], bxb[u:u + D, h // 2, :], wsl[u:u + D, :],
                                 start=True, stop=True)
                if h == H - 2:
                    last.then_inc(pe_step, 1)
            last.then_inc(wxs_m, 1)
            pe.wait_ge(plan_cnt, 1)
            pe.transpose(ps[0:1, 1, 64:64 + NW + 1], col[0:NW + 1, 3:4], ident[0:NW + 1, 0:NW + 1]).then_inc(plan_t, 1)
            pe.wait_ge(plan_done, 2)
            general = pe.value_load(flag_i[0:1, 0:1], min_val=0, max_val=1)
            with pe.If(general):
                pe.sem_inc(gen_mm, 2)
                pe.wait_ge(wxs_c, 3)
                with pe.Fori(0, NG) as g:
                    pe.wait_ge(gen_sum, g * GW + 1)
                    for b in gen_bank:
                        pe.matmul(ps[:, b, :], zeros[:, 0:P], zeros, start=True, stop=False)
                    with pe.Fori(0, ROUNDS) as r:
                        n = g * ROUNDS + r
                        for i, b in enumerate(gen_bank):
                            pe.wait_ge(gen_hot, n * GW + i + 1)
                            if i == 0:
                                for k in range(3):
                                    pe.wait_ge(gen_rows[k], n * (16 * CH // 3) + 16 * CH // 3)
                            for j in range(CH):
                                last = pe.matmul(ps[0:WN, b, :], oneh[:, i % 2, j, 0:WN], ring[:, 0, j, :],
                                                 start=False, stop=False, skip_group_check=True)
                            last.then_inc(gen_mm, 1)
                    for b in gen_bank:
                        last = pe.matmul(ps[:, b, :], zeros[:, 0:P], zeros, start=False, stop=True)
                    last.then_inc(gen_zero, 1)

            for n in range(MT):
                s = n % (MT // 2)
                pe.wait_ge(ld_wih, 16 * (MT // 2) * (1 + n // (MT // 2)))
                if n < 2:
                    pe.wait_ge(wxs_c, 3)
                else:
                    pe.wait_ge(wprep_h, n)
                    pe.wait_ge(wprep_l, n)
                for k in range(KT):
                    last = pe.transpose(ps[:, XA + n % 2, k * P:(k + 1) * P], raw[:, s * HID + k * P:s * HID + (k + 1) * P],
                                        ident[:, :])
                last.then_inc(wprep_t, 1)

            def sums_of(p, e):
                pe.wait_ge(hot_done[e], p + 1)
                for j in range(CH):
                    if j % HALF == 0:
                        pe.wait_ge(rows_in[e][j // HALF], 16 * HALF * p + 16 * HALF)
                    last = pe.matmul(ps[0:WN, SUM_A + e, :], oneh[:, e, j, 0:WN], ring[:, e, j, :],
                                     start=(j == 0), stop=(j == CH - 1))
                    if j == HALF - 1:
                        last.then_inc(half_used[e], 1)
                last.then_inc(sum_done[e], 1)

            def transpose_x(p, swt_before):
                for e in range(2):
                    pe.wait_ge(agg_done[e], p + 1)
                pe.wait_ge(xn_in, 32 * p + 32)
                if swt_before is not None:
                    after(pe, swt_done, swt_before)
                for e in range(2):
                    for q in range(2):
                        for hh in range(CT):
                            pe.transpose(xx16[:, hh, q, e * P:e * P + WN],
                                         xn16[0:WN, e, q * C + hh * P:q * C + (hh + 1) * P], ident16[0:WN, 0:WN])
                    for hh in range(CT):
                        last = pe.transpose(ps[:, XA, hh * 256 + e * P:hh * 256 + e * P + WN],
                                            agg[0:WN, e, hh * P:(hh + 1) * P], ident[0:WN, 0:WN])
                last.then_inc(xt_done, 1)

            def graph_layer(p):
                pe.wait_ge(xsplit_a, 5 * p + 5)
                pe.wait_ge(xsplit_v, p + 1)
                after(pe, gate_act, MT * p)
                for m in range(KT):
                    dst = ps[:, HA + m // 2, (m % 2) * 256:(m % 2) * 256 + 256]
                    for k in range(2 * CT):
                        xh, xl = ((at_h, at_l), (xt_h, xt_l))[k // CT]
                        last = three(pe, dst, w1_h[:, k, m * P:(m + 1) * P], w1_l[:, k, m * P:(m + 1) * P],
                                     xh[:, k % CT, :], xl[:, k % CT, :], k == 0, k == 2 * CT - 1)
                    if m % 2:
                        last.then_inc(h_mm, 1)

            def transpose_x2(p):
                pe.wait_ge(x2_norm, 2 * p + 2)
                for e in range(2):
                    for hh in range(CT):
                        last = pe.transpose(ps[:, XX, hh * 256 + e * P:hh * 256 + e * P + WN],
                                            x2[0:WN, e, hh * P:(hh + 1) * P], ident[0:WN, 0:WN])
                last.then_inc(x2t_mm, 1)

            def logits(p):
                pe.wait_ge(x2t_hi, p + 1)
                pe.wait_ge(x2t_lo, p + 1)
                for e in range(2):
                    for hh in range(CT):
                        dst = ps[0:WN, XA + e, :]
                        c = slice(e * P, e * P + WN)
                        last = three(pe, dst, x2t_h[:, hh, c], x2t_l[:, hh, c], wxs_h[:, hh, :], wxs_l[:, hh, :],
                                     hh == 0, hh == CT - 1)
                    last.then_inc(lg_mm, 1)

            def cell_gates(p, n0, n1):
                if n0 == 0:
                    pe.wait_ge(h_hi, 2 * p + 2)
                    pe.wait_ge(h_lo, 2 * p + 2)
                for n in range(n0, n1):
                    s = n % 4
                    if n >= 4 and n % 2 == 0:
                        pe.wait_ge(gate_act, MT * p + n - 2)
                    dst = ps[:, HA + s // 2, (s % 2) * 256:(s % 2) * 256 + 256]
                    for k in range(KT):
                        last = three(pe, dst, wih_h[:, k, n, :], wih_l[:, k, n, :], h_h[:, k, :], h_l[:, k, :],
                                     k == 0, k == KT - 1)
                    if n % 2:
                        last.then_inc(gate_mm, 1)

            def token_sums(p):
                pe.wait_ge(sw_done, p + 1)
                for e in range(2):
                    for j in range(KT):
                        last = pe.transpose(ps[:, XA + e, j * P:j * P + WN], sw[0:WN, e, j * P:(j + 1) * P], ident[0:WN, 0:WN])
                    last.then_inc(swt_mm, 1)
                pe.wait_ge(x2_hi, p + 1)
                pe.wait_ge(x2_lo, p + 1)
                pe.wait_ge(sw_hi, p + 1)
                pe.wait_ge(sw_lo, p + 1)
                for hh in range(CT):
                    for e in range(2):
                        c = slice(hh * P, (hh + 1) * P)
                        for i, (wx, s) in enumerate(((x2_h, sw_h), (x2_h, sw_l), (x2_l, sw_h))):
                            end = isinstance(p, int) and p == NP - 1 and e == 1 and i == 2
                            last = pe.matmul(ps[:, TOK + hh, :], wx[0:WN, e, c], s[0:WN, e, :], start=False, stop=end,
                                             skip_group_check=not end)
                last.then_inc(tok_mm, 1)

            def out_layer(p, sums_before):
                pe.wait_ge(hl_hi, 2 * p + 2)
                pe.wait_ge(hl_lo, 2 * p + 2)
                pe.wait_ge(agg_done[1], sums_before)
                for e in range(2):
                    for k in range(KT):
                        c = slice(e * P, e * P + WN)
                        last = three(pe, ps[0:WN, SUM_B, e * C:(e + 1) * C], hl_h[:, k, c], hl_l[:, k, c],
                                     wfc_h[:, k, :], wfc_l[:, k, :], k == 0, k == KT - 1)
                last.then_inc(y_mm, 1)

            def turn(t, gather, gnn, ffn, ahead):
                if gnn:
                    transpose_x(t - 1, 2 * (t - 2) if ffn else None)
                if ffn:
                    out_layer(t - 2, t if gnn else NP)
                if gnn:
                    graph_layer(t - 1)
                if gather:
                    sums_of(t, 0)
                if ffn:
                    transpose_x2(t - 2)
                if gnn:
                    if isinstance(t, int) and t == 1:
                        pe.wait_ge(wprep_h, MT + 2)
                        pe.wait_ge(wprep_l, MT + 2)
                    cell_gates(t - 1, 0, 4)
                if ffn:
                    logits(t - 2)
                if gnn and not ffn:
                    cell_gates(t - 1, 4, MT)
                if gather:
                    if ffn:
                        pe.wait_ge(x2_step, 4 * (t - 2) + 1)
                    sums_of(t, 1)
                if gnn and ffn:
                    cell_gates(t - 1, 4, MT)
                if ffn:
                    token_sums(t - 2)

            lo, hi = turns(turn)
            with pe.Fori(lo, hi) as t:
                turn(t, True, True, True, True)
            last_turns(turn)

            for k in range(FB):
                pe.sem_inc(f_mm[k], 1)
            pe.wait_ge(norm_add, 2 * NP)
            for h in range(H):
                last = pe.matmul(ps[0:G, 0, h:h + 1], norm[0:WN, h * G:(h + 1) * G], ones[0:WN, 0:1], start=True, stop=True)
            last.then_inc(att_pe, 1)
            pe.wait_ge(ld_att, 16 * 6)
            pe.wait_ge(att_v, V_TKS)
            for h in range(H):
                c = slice(h * G, (h + 1) * G)
                for ct in range(CT):
                    last = pe.matmul(ps[0:G, 1, c], tks[:, ct, c], wfx[:, ct, c], start=(ct == 0), stop=(ct == CT - 1))
            last.then_inc(att_pe, 1)
            pe.wait_ge(att_v, V_TOKENS)
            for h in range(H):
                c = slice(h * G, (h + 1) * G)
                last = pe.transpose(ps[0:G, 2, c], tokens[:, c], ident[0:G, 0:G])
            last.then_inc(att_pe, 1)
            pe.wait_ge(att_v, V_TOKT)
            pe.matmul(ps[0:D, 3, :], wqkv[:, 0, :], tokt[:, :], start=True, stop=True)
            pe.matmul(ps[0:D, 4, :], wqkv[:, 1, :], tokt[:, :], start=True, stop=True).then_inc(att_pe, 1)
            for h in range(H):
                c = slice(h * G, (h + 1) * G)
                last = pe.matmul(ps[0:G, 5, c], tokt[:, c], wqkv[:, 2, :], start=True, stop=True)
            last.then_inc(att_pe, 1)
            pe.wait_ge(att_v, V_QK)
            for h in range(H):
                c = slice(h * G, (h + 1) * G)
                last = pe.matmul(ps[0:G, 0, c], qt[:, c], kt[:, c], start=True, stop=True)
            last.then_inc(att_pe, 1)
            pe.wait_ge(att_v, V_ATT)
            for h in range(H):
                c = slice(h * G, (h + 1) * G)
                last = pe.transpose(ps[0:G, 1, c], att[:, c], ident[0:G, 0:G])
            last.then_inc(att_pe, 1)
            pe.wait_ge(att_v, V_ATTT)
            for h in range(H):
                c = slice(h * G, (h + 1) * G)
                last = pe.matmul(ps[0:D, 2, c], vv[:, c], attt[:, c], start=True, stop=True)
            last.then_inc(att_pe, 1)
            pe.wait_ge(att_v, V_OST)
            for h in range(H):
                u, j = (h % 2) * G, h // 2
                last = pe.matmul(ps[u:u + G, 3 + j // 2, (j % 2) * C:(j % 2) * C + C], ost[:, h * G:(h + 1) * G],
                                 wout[:, h, :], start=True, stop=True, skip_group_check=True)
            last.then_inc(att_pe, 1)
            pe.wait_ge(att_a, 3)
            pe.wait_ge(att_v, V_VLO)

            def f_mul(n, k):
                pe.wait_ge(f_hi[k], n + 1)
                pe.wait_ge(f_lo[k], n + 1)
                pe.wait_ge(f_out[k], n + 1)
                sh, sl = (x[k].rearrange("p (e j n) -> p e j n", e=2, j=KT) for x in (fsw_h, fsw_l))
                for e in range(2):
                    for j in range(KT):
                        last = three(pe, ps[0:WN, f_bank[k], e * C:(e + 1) * C], sh[:, e, j, :], sl[:, e, j, :],
                                     v_h[:, j, :], v_l[:, j, :], j == 0, j == KT - 1)
                last.then_inc(f_mm[k], 1)

            with pe.Fori(0, FN) as n:
                for k in range(FB):
                    f_mul(n, k)
            f_mul(FN, 0)

        @block.vector
        def _(dve):
            steps = [0]

            def link(ins):
                steps[0] += 1
                ins.then_inc(dve_step, 1)
                dve.wait_ge(dve_step, steps[0])

            dve.wait_ge(consts, NCONST)
            dve.tensor_copy(ident16[:, :], ident[:, :]).then_inc(w_ready, 1)

            def ln_stats(k):
                n, rows = (P, LR) if k < NCH else (REST, 1)
                q = k % 2
                dve.wait_ge(ln_in[k % 3], 16 * (k // 3 + 1))
                for r in range(rows):
                    steps[0] += 1
                    dve.bn_stats(stats[0:n, q, r, :], lx[k % 3][0:n, r, :]).then_inc(dve_step, 1)
                dve.wait_ge(dve_step, steps[0])
                for r in range(rows):
                    last = dve.bn_aggr(mv[0:n, q, r, :], stats[0:n, q, r, :])
                last.then_inc(ln_var, 1)

            def ln_scale(k):
                n, rows = (P, LR) if k < NCH else (REST, 1)
                q = k % 2
                dve.wait_ge(ln_sd, k + 1)
                link(dve.reciprocal(rstd[0:n, q, 0:rows], sd[0:n, q, 0:rows]))
                dve.scalar_tensor_tensor(out=nmr[0:n, q, 0:rows], in0=mv[0:n, q, 0:rows, 0], scalar=-1.0,
                                         in1=rstd[0:n, q, 0:rows], op0=ALU.mult, op1=ALU.mult).then_inc(ln_rstd, 1)

            def plan_a():
                dve.wait_ge(ld_tab, 32)
                link(dve.tensor_copy(edge_f[0:WN, 0:1], edge_i[0:WN, 0:1]))
                dve.tensor_scalar(pick[0:WN, 0:NW + 1], wbase[0:WN, 0:NW + 1], edge_f[0:WN, 0:1], None,
                                  ALU.is_gt).then_inc(plan_m, 1)
                link(dve.tensor_tensor(edge_le[0:WN, :], edge_i[0:WN, 0:ER], edge_i[0:WN, 1:ER + 1], ALU.is_le))
                dve.tensor_reduce(col[0:WN, 0:1], edge_le[0:WN, :], AX.X, ALU.add).then_inc(plan_m, 1)

            def plan_b():
                dve.wait_ge(plan_pw, 1)
                link(dve.tensor_scalar(col[0:NW + 1, 1:2], ps[0:NW + 1, 0, 0:1], 1.0, 0.0, ALU.subtract, ALU.max))
                dve.tensor_copy(coli[0:NW + 1, :], col[0:NW + 1, 1:2]).then_inc(plan_row, 1)

            def plan_c():
                dve.wait_ge(ld_rows, 16)
                link(dve.tensor_scalar(edge_le[0:NW + 1, :], edge_i[0:NW + 1, 0:ER], col[0:NW + 1, 7:8], None, ALU.is_lt))
                link(dve.tensor_reduce(col[0:NW + 1, 2:3], edge_le[0:NW + 1, :], AX.X, ALU.add))
                dve.scalar_tensor_tensor(out=col[0:NW + 1, 3:4], in0=col[0:NW + 1, 1:2], scalar=float(ER),
                                         in1=col[0:NW + 1, 2:3], op0=ALU.mult, op1=ALU.add).then_inc(plan_cnt, 1)

            def plan_d():
                dve.wait_ge(plan_t, 1)
                link(dve.tensor_copy(row[:, 0, 0:NW + 1], ps[0:1, 1, 64:64 + NW + 1]))
                link(dve.tensor_tensor(row[:, 1, 0:NW], row[:, 0, 1:NW + 1], row[:, 0, 0:NW], ALU.subtract))
                link(dve.tensor_reduce(row[:, 2, 0:1], row[:, 1, 0:NW], AX.X, ALU.max))
                link(dve.tensor_scalar(row[:, 2, 1:2], row[:, 2, 0:1], float(CAP), None, ALU.is_gt))
                link(dve.tensor_scalar(row[:, 2, 2:3], ps[0:1, 1, 0:1], float(E), None, ALU.is_lt))
                link(dve.tensor_tensor(row[:, 2, 3:4], row[:, 2, 1:2], row[:, 2, 2:3], ALU.max))
                dve.tensor_copy(flag_i[:, :], row[:, 2, 3:4]).then_inc(plan_done, 1)
                link(dve.tensor_scalar(row[:, 3, 0:NW], row[:, 0, 0:NW], -1.0, float(E), ALU.mult, ALU.add))
                link(dve.tensor_scalar(row[:, 4, 0:NW], row[:, 3, 0:NW], row[:, 2, 3:4], None, ALU.mult))
                dve.tensor_tensor(base_i[:, 0:NW], row[:, 0, 0:NW], row[:, 4, 0:NW], ALU.add).then_inc(plan_done, 1)

            def bias_rows():
                dve.wait_ge(ld_small, 16 * (1 + 6 + 1 + 3 + 1 + 2))
                link(dve.tensor_scalar(rtemp[:, :], temp8[:, :], 0.1, 5.0, ALU.max, ALU.min))
                link(dve.reciprocal(rtemp[:, :], rtemp[:, :]))
                for g in range(3):
                    link(dve.tensor_tensor(bgate[:, :, g], braw[:, 0, g, :], braw[:, 1, g, :], ALU.add))
                for g in (0, 2):
                    link(dve.tensor_scalar(bgate[:, :, g], bgate[:, :, g], 0.5, None, ALU.mult))
                link(dve.tensor_copy(bxb, bxc.unsqueeze(2).to_broadcast([P, KT, P])))
                dve.wait_ge(wxt_t, 1)
                wx4 = wxt.rearrange("p a b -> p (a b)").rearrange("p (c n) -> p c n", c=CT)
                dve.tensor_copy(wx4, ps[:, XA:XA + 2, :]).then_inc(wxt_c, 2)

            def slice_weights():
                dve.wait_ge(wxs_m, 1)
                for ct in range(CT):
                    dve.tensor_tensor(sw[:, ct, :].rearrange("p (h g) -> p h g", g=G),
                                      ps[:, HA + ct, :].rearrange("p (h g) -> p h g", g=G),
                                      rtemp[:, :].unsqueeze(2).to_broadcast([P, H, G]), ALU.mult).then_inc(wxs_c, 1)
                b3 = biasx[:, :].rearrange("p (h g) -> p h g", g=G)
                link(dve.tensor_tensor(b3, ps[:, XA, :].rearrange("p (h g) -> p h g", g=G),
                                       bsl.unsqueeze(1).to_broadcast([P, H, G]), ALU.add))
                dve.tensor_tensor(b3, b3, rtemp[:, :].unsqueeze(2).to_broadcast([P, H, G]), ALU.mult).then_inc(wxs_c, 1)
                dve.wait_ge(wprep_h, 1)
                dve.wait_ge(wxs_c, 2)
                dve.tensor_tensor(wxs_l[:, :, :], sw[:, :, :], wxs_h[:, :, :].bitcast(F32), ALU.subtract).then_inc(wprep_l, 1)

            ln_stats(0)
            for k in range(NCH + 1):
                ln_scale(k)
                if k < NCH:
                    ln_stats(k + 1)
                if k % 2:
                    ln_low(dve, k - 1)
                if k == 1:
                    plan_a()
                if k == 3:
                    plan_b()
                if k == 6:
                    bias_rows()
                if k == 8:
                    plan_c()
                if k == 10:
                    plan_d()
            ln_low(dve, NCH - 1)
            ln_low(dve, NCH)
            dve.wait_ge(w1_free, 1)
            dve.tensor_tensor(w1_l[:, :, :], raw[:, 0:4 * HID].rearrange("p (k n) -> p k n", n=HID),
                              w1_h[:, :, :].bitcast(F32), ALU.subtract).then_inc(w1_free, 1)
            slice_weights()
            general = dve.value_load(flag_i[0:1, 0:1], min_val=0, max_val=1)

            def one_hots(e, idx, base, rel_sem, rel_n, hot_sem):
                dve.tensor_scalar(rel[:, e, :], didx[:, idx, :], base, None, ALU.subtract).then_inc(rel_sem, 1)
                dve.wait_ge(rel_sem, rel_n)
                for j in range(CH):
                    last = dve.tensor_scalar(oneh[:, e, j, 0:WN], iota[:, 0:WN], rel[:, e, j:j + 1], None, ALU.is_equal)
                last.then_inc(hot_sem, 1)

            with dve.If(general):
                dve.sem_inc(gen_sum, 1)
                with dve.Fori(0, NG) as g:
                    with dve.Fori(0, ROUNDS) as r:
                        n = g * ROUNDS + r
                        for i in range(GW):
                            if i == 0:
                                dve.wait_ge(gen_idx, n * 32 + 32)
                            if i != 1:
                                dve.wait_ge(gen_mm, n * GW + max(i + 1, 2))
                            one_hots(i % 2, 0, wbase[:, ds(g * GW + i, 1)], gen_rel, n * GW + i + 1, gen_hot)
                    dve.wait_ge(gen_zero, g + 1)
                    for i, b in enumerate(gen_bank):
                        dve.wait_ge(gen_st, (g * GW + i) * 16 + 16)
                        dve.tensor_copy(agg[0:WN, 1, :], ps[0:WN, b, 0:C]).then_inc(gen_high, 1)
                        dve.wait_ge(gen_high, g * GW + i + 1)
                        dve.tensor_tensor(agg[0:WN, 0, :], agg[0:WN, 1, :], ps[0:WN, b, C:2 * C],
                                          ALU.add).then_inc(gen_sum, 1)

            def hots(p, e):
                dve.wait_ge(idx_in[e], 32 * p + 32)
                after(dve, sum_done[e], p)
                one_hots(e, e, wbase[:, ds(2 * p + e, 1)], rel_done[e], p + 1, hot_done[e])

            def add_halves(p, e):
                dve.wait_ge(sum_done[e], p + 1)
                after(dve, xt_done, p)
                dve.tensor_copy(agg[0:WN, e, :], ps[0:WN, SUM_A + e, C:2 * C]).then_inc(low_out[e], 1)
                with dve.If(general):
                    dve.wait_ge(gen_in, 32 * p + 32)
                    dve.wait_ge(low_out[e], p + 1)
                    dve.tensor_tensor(agg[0:WN, e, :], agg[0:WN, e, :], extra[0:WN, e, :], ALU.add).then_inc(gen_add, 1)
                    dve.wait_ge(gen_add, 2 * p + e + 1)
                    dve.tensor_tensor(agg[0:WN, e, :], agg[0:WN, e, :], ps[0:WN, SUM_A + e, 0:C],
                                      ALU.add).then_inc(agg_done[e], 1)
                with dve.Else():
                    dve.wait_ge(low_out[e], p + 1)
                    dve.tensor_tensor(agg[0:WN, e, :], agg[0:WN, e, :], ps[0:WN, SUM_A + e, 0:C],
                                      ALU.add).then_inc(agg_done[e], 1)

            def split_x(p):
                dve.wait_ge(xsplit_a, 5 * p + 1)
                dve.tensor_tensor(valid(at_l[:, :, :]), bank_valid(XA), valid(at_h[:, :, :]).bitcast(F32),
                                  ALU.subtract).then_inc(xsplit_v, 1)

            def norm_x2(p):
                dve.wait_ge(y_mm, p + 1)
                dve.wait_ge(x_in, 32 * p + 32)
                after(dve, x2t_mm, p)
                after(dve, x2_hi, p)
                y = ps[0:WN, SUM_B, :].rearrange("p (e c) -> p e c", e=2)
                dve.tensor_tensor(x2[0:WN, :, :], y, xin[0:WN, :, :], ALU.add).then_inc(x2_step, 1)
                dve.wait_ge(x2_step, 4 * p + 1)
                dve.tensor_tensor(x2[0:WN, :, :], x2[0:WN, :, :], bfc[0:WN, :].unsqueeze(1).to_broadcast([WN, 2, C]),
                                  ALU.add).then_inc(x2_step, 1)
                dve.wait_ge(x2_step, 4 * p + 2)
                for e in range(2):
                    dve.bn_stats(stats[0:WN, 0, e, :], x2[0:WN, e, :]).then_inc(x2_step, 1)
                dve.wait_ge(x2_step, 4 * p + 4)
                dve.tensor_tensor(xin[0:WN, :, :], x2[0:WN, :, :], bout[0:WN, :].unsqueeze(1).to_broadcast([WN, 2, C]),
                                  ALU.add).then_inc(res_done, 1)
                for e in range(2):
                    dve.bn_aggr(mv[0:WN, 0, e, :], stats[0:WN, 0, e, :]).then_inc(var_done, 1)
                dve.wait_ge(sd_done, p + 1)
                dve.reciprocal(rstd[0:WN, 0, 0:2], sd[0:WN, 0, 0:2]).then_inc(rstd_done, 1)
                dve.wait_ge(rstd_done, 2 * p + 1)
                dve.scalar_tensor_tensor(out=nmr[0:WN, 0, 0:2], in0=mv[0:WN, 0, 0:2, 0], scalar=-1.0,
                                         in1=rstd[0:WN, 0, 0:2], op0=ALU.mult, op1=ALU.mult).then_inc(rstd_done, 1)

            def low_x2(p):
                dve.wait_ge(x2_hi, p + 1)
                after(dve, tok_mm, p)
                dve.tensor_tensor(x2_l[0:WN, :, :], x2[0:WN, :, :], x2_h[0:WN, :, :].bitcast(F32),
                                  ALU.subtract).then_inc(x2_lo, 1)

            def low_h(p, q):
                dve.wait_ge(h_hi, 2 * p + q + 1)
                dve.tensor_tensor(h_l[:, 2 * q:2 * q + 2, :], hf[:, 2 * q:2 * q + 2, :],
                                  h_h[:, 2 * q:2 * q + 2, :].bitcast(F32), ALU.subtract).then_inc(h_lo, 1)

            def low_x2t(p):
                dve.wait_ge(x2t_hi, p + 1)
                dve.tensor_tensor(valid(x2t_l[:, :, :]), bank_valid(XX), valid(x2t_h[:, :, :]).bitcast(F32),
                                  ALU.subtract).then_inc(x2t_lo, 1)

            def heads(x):
                return x[0:WN, :, :].rearrange("p e (h g) -> p (e h) g", g=G)

            def softmax(p):
                dve.wait_ge(lg_mm, 2 * p + 2)
                after(dve, swt_mm, 2 * p)
                after(dve, sw_hi, p)
                dve.tensor_tensor(sw[0:WN, :, :], ps[0:WN, XA:XA + 2, :],
                                  biasx[0:WN, :].unsqueeze(1).to_broadcast([WN, 2, HG]), ALU.add).then_inc(sm_step, 1)
                dve.wait_ge(sm_step, 4 * p + 1)
                dve.tensor_reduce(mx8[0:WN, :], heads(sw), AX.X, ALU.max).then_inc(sm_step, 1)
                dve.wait_ge(sm_step, 4 * p + 2)
                dve.tensor_tensor(heads(sw), heads(sw), mx8[0:WN, :].unsqueeze(2).to_broadcast([WN, 2 * H, G]),
                                  ALU.subtract).then_inc(lg_sub, 1)

            def softmax_end(p):
                dve.wait_ge(lg_exp, p + 1)
                dve.tensor_reduce(sm8[0:WN, :], heads(sw), AX.X, ALU.add).then_inc(sm_step, 1)
                dve.wait_ge(sm_step, 4 * p + 3)
                dve.reciprocal(rs8[0:WN, :], sm8[0:WN, :]).then_inc(sm_step, 1)
                dve.wait_ge(sm_step, 4 * p + 4)
                dve.tensor_tensor(heads(sw), heads(sw), rs8[0:WN, :].unsqueeze(2).to_broadcast([WN, 2 * H, G]),
                                  ALU.mult).then_inc(sw_done, 1)
                dve.wait_ge(sw_done, p + 1)
                for e in range(2):
                    after(dve, norm_add, 2 * p + e)
                    dve.tensor_tensor(norm[0:WN, :], norm[0:WN, :], sw[0:WN, e, :], ALU.add).then_inc(norm_add, 1)

            def low_sw(p):
                dve.wait_ge(sw_hi, p + 1)
                after(dve, tok_mm, p)
                dve.tensor_tensor(sw_l[0:WN, :, :], sw[0:WN, :, :], sw_h[0:WN, :, :].bitcast(F32),
                                  ALU.subtract).then_inc(sw_lo, 1)

            def cell_c(p, f):
                dve.wait_ge(gate_act, MT * p + 3 * f + 3)
                dve.scalar_tensor_tensor(out=gate[:, 0, f, :], in0=gate[:, 0, f, :], scalar=1.0, in1=gate[:, 1, f, :],
                                         op0=ALU.add, op1=ALU.mult).then_inc(cell_v, 1)

            def cell_o(p, f):
                dve.wait_ge(cell_t, KT * p + f + 1)
                dve.scalar_tensor_tensor(out=hf[:, f, :], in0=gate[:, 2, f, :], scalar=1.0, in1=gate[:, 1, f, :],
                                         op0=ALU.add, op1=ALU.mult).then_inc(cell_out, 1)

            def low_hl(p, q):
                if q == 0:
                    after(dve, y_mm, p)
                dve.wait_ge(hl_hi, 2 * p + q + 1)
                dve.tensor_tensor(hl_l[:, 2 * q:2 * q + 2, :], hf[:, 2 * q:2 * q + 2, :],
                                  hl_h[:, 2 * q:2 * q + 2, :].bitcast(F32), ALU.subtract).then_inc(hl_lo, 1)

            def turn(t, gather, gnn, ffn, ahead):
                if gnn:
                    split_x(t - 1)
                if ffn:
                    norm_x2(t - 2)
                if gnn:
                    low_h(t - 1, 0)
                    low_h(t - 1, 1)
                if ffn:
                    low_x2(t - 2)
                if gather:
                    add_halves(t, 0)
                if ffn:
                    low_x2t(t - 2)
                if ahead:
                    hots(t + 1, 0)
                if gnn:
                    cell_c(t - 1, 0)
                    cell_o(t - 1, 0)
                if ffn:
                    softmax(t - 2)
                if not (gnn and not ffn):
                    if gather:
                        add_halves(t, 1)
                    if ahead:
                        hots(t + 1, 1)
                if gnn:
                    cell_c(t - 1, 1)
                if ffn:
                    softmax_end(t - 2)
                if gnn:
                    cell_o(t - 1, 1)
                    cell_c(t - 1, 2)
                if ffn:
                    low_sw(t - 2)
                if gnn:
                    cell_o(t - 1, 2)
                    cell_c(t - 1, 3)
                    cell_o(t - 1, 3)
                    low_hl(t - 1, 0)
                    low_hl(t - 1, 1)
                if gnn and not ffn:
                    add_halves(t, 1)
                    hots(t + 1, 1)

            hots(0, 0)
            for n in range(MT):
                if n == MT // 2:
                    hots(0, 1)
                dve.wait_ge(wprep_h, n + 2)
                dve.tensor_tensor(wih_l[:, :, n, :], ps[:, XA + n % 2, :].rearrange("p (k m) -> p k m", m=P),
                                  wih_h[:, :, n, :].bitcast(F32), ALU.subtract).then_inc(wprep_l, 1)
            dve.wait_ge(wprep_h, MT + 2)
            dve.scalar_tensor_tensor(out=wfc_l[:, :, :], in0=raw[:, 0:KT * C].rearrange("p (k n) -> p k n", n=C),
                                     scalar=0.5, in1=wfc_h[:, :, :].bitcast(F32), op0=ALU.mult,
                                     op1=ALU.subtract).then_inc(wprep_l, 1)
            lo, hi = turns(turn)
            with dve.Fori(lo, hi) as t:
                turn(t, True, True, True, True)
            last_turns(turn)

            def f_low(n, k):
                dve.wait_ge(f_hi[k], n + 1)
                dve.tensor_tensor(fsw_l[k], fsw[k], fsw_h[k].bitcast(F32), ALU.subtract).then_inc(f_lo[k], 1)

            count = [0]

            def step(ins, wait=True):
                count[0] += 1
                ins.then_inc(att_v, 1)
                if wait:
                    dve.wait_ge(att_v, count[0])

            def hd(x):
                return x.rearrange("p (h g) -> p h g", h=H)

            def spread(x):
                return x.unsqueeze(2).to_broadcast([G, H, D])

            dve.wait_ge(tok_mm, NP)
            dve.wait_ge(sum_done[1], NP)
            step(dve.tensor_copy(tks, ps[:, TOK:TOK + 2, :]))
            assert count[0] == V_TKS
            dve.wait_ge(att_pe, 1)
            nc8, rn8, nr8 = mx8[0:G, 0:H], rs8[0:G, 0:H], sm8[0:G, 0:H]
            step(dve.tensor_scalar(nc8, ps[0:G, 0, 0:H], 1e-5, None, ALU.add))
            step(dve.reciprocal(rn8, nc8))
            step(dve.tensor_tensor(nr8, ps[0:G, 0, 0:H], rn8, ALU.mult))
            dve.wait_ge(ld_att, 16 * 6)
            step(dve.tensor_tensor(hd(tmp), hd(bfx), spread(nr8), ALU.mult))
            dve.wait_ge(att_pe, 2)
            step(dve.tensor_tensor(hd(tokens), hd(ps[0:G, 1, :]), spread(rn8), ALU.mult))
            step(dve.tensor_tensor(tokens, tokens, tmp, ALU.add))
            assert count[0] == V_TOKENS
            dve.wait_ge(att_pe, 3)
            step(dve.tensor_copy(tokt, ps[0:G, 2, :]))
            assert count[0] == V_TOKT
            dve.wait_ge(att_pe, 4)
            for x, b in ((qt, 3), (kt, 4)):
                step(dve.tensor_copy(x, ps[0:G, b, :]), False)
            assert count[0] == V_QK
            dve.wait_ge(att_pe, 6)
            step(dve.tensor_reduce(mx8[0:G, 0:H], hd(ps[0:G, 0, :]), AX.X, ALU.max))
            step(dve.tensor_tensor(hd(att), hd(ps[0:G, 0, :]), spread(mx8[0:G, 0:H]), ALU.subtract))
            assert count[0] == ATT_SUB
            dve.wait_ge(att_a, 1)
            step(dve.tensor_reduce(sm8[0:G, 0:H], hd(att), AX.X, ALU.add))
            step(dve.reciprocal(rs8[0:G, 0:H], sm8[0:G, 0:H]))
            step(dve.tensor_tensor(hd(att), hd(att), spread(rs8[0:G, 0:H]), ALU.mult))
            assert count[0] == V_ATT
            step(dve.tensor_copy(vv, ps[0:G, 5, :]), False)
            assert count[0] == V_V
            dve.wait_ge(att_pe, 7)
            step(dve.tensor_copy(attt, ps[0:G, 1, :]))
            assert count[0] == V_ATTT
            dve.wait_ge(att_pe, 8)
            step(dve.tensor_copy(ost, ps[0:G, 2, :]))
            assert count[0] == V_OST
            f_low(0, 0)
            for b in range(2):
                dve.wait_ge(att_a, 2 + b)
                step(dve.tensor_tensor(v_l[:, 2 * b:2 * b + 2, :], ps[:, 3 + b, :].rearrange("p (j c) -> p j c", c=C),
                                       v_h[:, 2 * b:2 * b + 2, :].bitcast(F32), ALU.subtract), False)
            assert count[0] == V_VLO

            def f_add(n, k):
                dve.wait_ge(f_mm[k], n + 2)
                dve.wait_ge(f_res[k], 32 * n + 32)
                after(dve, f_st[k], 32 * n)
                dve.tensor_tensor(fo[k][0:WN], ps[0:WN, f_bank[k], :].rearrange("p (e c) -> p e c", e=2),
                                  fres[k][0:WN], ALU.add).then_inc(f_out[k], 1)

            for k in range(FB):
                dve.sem_inc(f_out[k], 1)

            def f_round(n):
                for k in range(FB):
                    f_low(n + (k + 1) // FB, (k + 1) % FB)
                    f_add(n, k)

            f_round(0)
            with dve.Fori(1, FN) as n:
                f_round(n)
            f_add(FN, 0)


_INS = ["x", "src", "dst", "W_rel", "b_rel", "W_root", "W_ih", "b_ih", "b_hh", "W_fc", "b_fc",
        "W_fx", "b_fx", "W_x", "b_x", "W_slice", "b_slice", "W_q", "W_k", "W_v", "W_out", "b_out", "temperature"]
_GNN = ("W_rel", "b_rel", "W_root", "W_ih", "b_ih", "b_hh", "W_fc", "b_fc")


def kernel(**inputs):
    import numpy as np
    from concourse import bacc
    from concourse.bass_utils import run_bass_kernel_spmd

    nc = bacc.Bacc("TRN2", target_bir_lowering=False, num_devices=1)
    arrays, args = {}, {}
    for name in _INS:
        full = name if name in ("x", "src", "dst") else ("L0_gnn_" if name in _GNN else "L0_ffn_") + name
        v = np.ascontiguousarray(inputs[full])
        arrays[f"in_{name}"] = v
        args[name] = nc.dram_tensor(f"in_{name}", v.shape, mybir.dt.from_np(v.dtype), kind="ExternalInput").ap()
    out = nc.dram_tensor("out_x", inputs["x"].shape, F32, kind="ExternalOutput").ap()
    build_program(nc, args, out)
    r = run_bass_kernel_spmd(nc, [arrays], core_ids=[0])
    return r.results[0]["out_x"]
```
